# Optimizing a Trainium2 kernel written in Bass

```python
import numpy as np
import jax
import jax.numpy as jnp

def _softmax(x, axis=-1):
    return jax.nn.softmax(x, axis=axis)

def _gelu(x):
    return jax.nn.gelu(x, approximate=True)

def _silu(x):
    return jax.nn.silu(x)

def _sigmoid(x):
    return jax.nn.sigmoid(x)

def _layernorm(x, axis=-1, eps=1e-05):
    m = jnp.mean(x, axis=axis, keepdims=True)
    v = jnp.var(x, axis=axis, keepdims=True)
    return (x - m) / jnp.sqrt(v + eps)

def _scatter_add(tgt, idx, src, axis=0):
    return tgt.at[idx].add(src)

def _segment_sum(src, seg, n):
    return jax.ops.segment_sum(src, seg, n)
kernel_name = 'mk_decoder_preln_d1_seqx_r8_112214'

def setup_inputs(seed: int=0):
    np.random.seed(seed)
    _w = jnp.asarray

    def _rec_inputs():
        import jax
        import jax.numpy as jnp
        _rk = jax.random.key(seed)
        x = 7.22e-05 + 1 * jax.random.normal(jax.random.fold_in(_rk, 1), (8, 128, 512), jnp.float32)
        _lenS = 128 - jax.random.randint(jax.random.fold_in(_rk, 7), (8,), 0, max(1, 128 // 4) + 1, jnp.int32)
        _lenS2 = 128 - jax.random.randint(jax.random.fold_in(_rk, 8), (8,), 0, max(1, 128 // 4) + 1, jnp.int32)
        _ctx_4096P = jax.random.normal(jax.random.fold_in(_rk, 11), (8, 16, 512), jnp.float32)
        _ctx_4096c = jax.random.dirichlet(jax.random.fold_in(_rk, 511), 0.3 * jnp.ones((16,), jnp.float32), (8, 128))
        _ctx_4096t = jnp.einsum('bsk,bkd->bsd', _ctx_4096c, _ctx_4096P)
        _ctx_4096t = _ctx_4096t * jax.lax.rsqrt(jnp.mean(jnp.square(_ctx_4096t)) + 1e-12) * 0.953939
        ctx_4096 = 4.13588e-05 + 0.999923 * (_ctx_4096t + 0.3 * jax.random.normal(jax.random.fold_in(_rk, 611), (8, 128, 512), jnp.float32))
        _validS = jnp.arange(128)[None, :] < _lenS[:, None]
        _validS2 = jnp.arange(128)[None, :] < _lenS2[:, None]
        _causal = jnp.tril(jnp.ones((128, 128), dtype=bool))
        mask_BxSxS2_bk0 = jnp.logical_not(jnp.broadcast_to(_validS2[:, None, :], (8, 128, 128)))
        return (x, ctx_4096, mask_BxSxS2_bk0)
    x, ctx_4096, mask_BxSxS2_bk0 = _rec_inputs()

    def _L0_attn_setup():
        import jax, jax.numpy as jnp
        import numpy as np
        from jax import lax
        H, KVH, D, CHUNK = (32, 8, 128, 128)
        ROPE_THETA = 10000.0
        RMS_EPS = 1e-05

        def _rope_tables(L):
            inv_freq = 1.0 / ROPE_THETA ** (jnp.arange(0, D, 2, dtype=jnp.float32) / D)
            ang = jnp.arange(L, dtype=jnp.float32)[:, None] * inv_freq
            cos = jnp.concatenate([jnp.cos(ang), jnp.cos(ang)], axis=-1)[:, None, :]
            sin = jnp.concatenate([jnp.sin(ang), jnp.sin(ang)], axis=-1)[:, None, :]
            return (cos, sin)

        def _apply_rope(x, cos, sin):
            half = D // 2
            rot = jnp.concatenate([-x[..., half:], x[..., :half]], axis=-1)
            return x * cos + rot * sin
        key = jax.random.key(seed)
        ks = jax.random.split(key, 10)
        B, L, HID = (1, 512, 512)
        s = lambda fan: 1.0 / np.sqrt(fan)
        return {'hidden_states': jax.random.normal(ks[0], (B, L, HID), jnp.float32), 'Wq': jax.random.normal(ks[1], (H * D, HID), jnp.float32) * s(HID), 'Wk': jax.random.normal(ks[2], (KVH * D, HID), jnp.float32) * s(HID), 'Wv': jax.random.normal(ks[3], (KVH * D, HID), jnp.float32) * s(HID), 'Wo': jax.random.normal(ks[4], (HID, H * D), jnp.float32) * s(H * D), 'Wg': jax.random.normal(ks[5], (H * D, HID), jnp.float32) * (s(HID) * 2 ** (-2.5)), 'Win': jax.random.normal(ks[6], (H, HID), jnp.float32) * s(HID), 'dt_bias': jnp.zeros((H,), jnp.float32), 'A_log_bias': jnp.log(jax.random.uniform(ks[7], (H,), jnp.float32, 1.0, 16.0)), 'gnorm_w': jnp.ones((D,), jnp.float32)}
    _L0_attn_all = _L0_attn_setup()
    _L0_attn_in = {k: v for k, v in _L0_attn_all.items() if k in ('Wq', 'Wk', 'Wv', 'Wo', 'Wg', 'Win', 'dt_bias', 'A_log_bias', 'gnorm_w')}
    del _L0_attn_all

    def _L0_xattn_setup():
        import jax, jax.numpy as jnp
        import numpy as np
        B, LQ, LK, D, H, DH = (2, 128, 128, 512, 32, 128)
        EPS = 1e-05

        def _rmsnorm(x, weight):
            var = jnp.mean(jnp.square(x), axis=-1, keepdims=True)
            return x * jax.lax.rsqrt(var + EPS) * weight
        key = jax.random.key(seed)
        ks = jax.random.split(key, 8)
        scale = 0.02
        return {'hidden_states': jax.random.normal(ks[0], (B, LQ, D), jnp.float32), 'key_value_states': jax.random.normal(ks[1], (B, LK, D), jnp.float32), 'attention_mask': jax.random.randint(ks[2], (B, LQ, LK), 0, 2) > 0, 'position_bias': jax.random.normal(ks[3], (H, LQ, LK), jnp.float32), 'ln_weight': jnp.ones((D,), jnp.float32), 'w_q': jax.random.normal(ks[4], (H * DH, D), jnp.float32) * scale, 'w_k': jax.random.normal(ks[5], (H * DH, D), jnp.float32) * scale, 'w_v': jax.random.normal(ks[6], (H * DH, D), jnp.float32) * scale, 'w_out': jax.random.normal(ks[7], (D, H * DH), jnp.float32) * scale}
    _L0_xattn_all = _L0_xattn_setup()
    _L0_xattn_in = {k: v for k, v in _L0_xattn_all.items() if k in ('position_bias', 'ln_weight', 'w_q', 'w_k', 'w_v', 'w_out')}
    del _L0_xattn_all

    def _L0_ffn_setup():
        import jax, jax.numpy as jnp
        import numpy as np
        HIDDEN = 512
        MOE_INTER = 128
        SHARED_INTER = 512
        NUM_EXPERTS = 16
        TOP_K = 2

        def _moe_forward(x, gate_w, w_gate_up, w_down, shared_w_gate_up, shared_w_down):
            orig_shape = x.shape
            x2 = x.reshape(-1, orig_shape[-1])
            gu_s = x2 @ shared_w_gate_up.T
            g_s, u_s = jnp.split(gu_s, 2, axis=-1)
            shared_out = jax.nn.silu(g_s) * u_s @ shared_w_down.T
            logits = x2 @ gate_w.T
            probs = jax.nn.softmax(logits, axis=-1)
            topk_vals, topk_idx = jax.lax.top_k(probs, TOP_K)
            topk_vals = topk_vals / jnp.sum(topk_vals, axis=-1, keepdims=True)
            combine = jnp.sum(jax.nn.one_hot(topk_idx, NUM_EXPERTS, dtype=x2.dtype) * topk_vals[..., None], axis=1)
            gu = jnp.einsum('th,eih->eti', x2, w_gate_up)
            g, u = jnp.split(gu, 2, axis=-1)
            act = jax.nn.silu(g) * u
            out_e = jnp.einsum('eti,ehi->eth', act, w_down)
            moe_out = jnp.einsum('eth,te->th', out_e, combine)
            return (moe_out + shared_out).reshape(orig_shape)
        key = jax.random.key(seed)
        ks = jax.random.split(key, 6)
        s = 0.02
        hidden_states = jax.random.normal(ks[0], (2, 256, HIDDEN), dtype=jnp.float32)
        gate_w = jax.random.normal(ks[1], (NUM_EXPERTS, HIDDEN), dtype=jnp.float32) * s
        w_gate_up = jax.random.normal(ks[2], (NUM_EXPERTS, 2 * MOE_INTER, HIDDEN), dtype=jnp.float32) * s
        w_down = jax.random.normal(ks[3], (NUM_EXPERTS, HIDDEN, MOE_INTER), dtype=jnp.float32) * s
        shared_w_gate_up = jax.random.normal(ks[4], (2 * SHARED_INTER, HIDDEN), dtype=jnp.float32) * s
        shared_w_down = jax.random.normal(ks[5], (HIDDEN, SHARED_INTER), dtype=jnp.float32) * s
        return {'hidden_states': hidden_states, 'gate_w': gate_w, 'w_gate_up': w_gate_up, 'w_down': w_down, 'shared_w_gate_up': shared_w_gate_up, 'shared_w_down': shared_w_down}
    _L0_ffn_all = _L0_ffn_setup()
    _L0_ffn_in = {k: v for k, v in _L0_ffn_all.items() if k in ('gate_w', 'w_gate_up', 'w_down', 'shared_w_gate_up', 'shared_w_down')}
    del _L0_ffn_all
    return {'x': x, 'ctx_4096': ctx_4096, 'mask_BxSxS2_bk0': mask_BxSxS2_bk0, 'L0_attn_Wq': _L0_attn_in['Wq'], 'L0_attn_Wk': _L0_attn_in['Wk'], 'L0_attn_Wv': _L0_attn_in['Wv'], 'L0_attn_Wo': _L0_attn_in['Wo'], 'L0_attn_Wg': _L0_attn_in['Wg'], 'L0_attn_Win': _L0_attn_in['Win'], 'L0_attn_dt_bias': _L0_attn_in['dt_bias'], 'L0_attn_A_log_bias': _L0_attn_in['A_log_bias'], 'L0_attn_gnorm_w': _L0_attn_in['gnorm_w'], 'L0_xattn_position_bias': _L0_xattn_in['position_bias'], 'L0_xattn_ln_weight': _L0_xattn_in['ln_weight'], 'L0_xattn_w_q': _L0_xattn_in['w_q'], 'L0_xattn_w_k': _L0_xattn_in['w_k'], 'L0_xattn_w_v': _L0_xattn_in['w_v'], 'L0_xattn_w_out': _L0_xattn_in['w_out'], 'L0_ffn_gate_w': _L0_ffn_in['gate_w'], 'L0_ffn_w_gate_up': _L0_ffn_in['w_gate_up'], 'L0_ffn_w_down': _L0_ffn_in['w_down'], 'L0_ffn_shared_w_gate_up': _L0_ffn_in['shared_w_gate_up'], 'L0_ffn_shared_w_down': _L0_ffn_in['shared_w_down']}

def reference(x, ctx_4096, mask_BxSxS2_bk0, L0_attn_Wq, L0_attn_Wk, L0_attn_Wv, L0_attn_Wo, L0_attn_Wg, L0_attn_Win, L0_attn_dt_bias, L0_attn_A_log_bias, L0_attn_gnorm_w, L0_xattn_position_bias, L0_xattn_ln_weight, L0_xattn_w_q, L0_xattn_w_k, L0_xattn_w_v, L0_xattn_w_out, L0_ffn_gate_w, L0_ffn_w_gate_up, L0_ffn_w_down, L0_ffn_shared_w_gate_up, L0_ffn_shared_w_down):
    import jax
    import jax.numpy as jnp

    def _L0_attn_ref(hidden_states, Wq, Wk, Wv, Wo, Wg, Win, dt_bias, A_log_bias, gnorm_w):
        import jax, jax.numpy as jnp
        import numpy as np
        from jax import lax
        H, KVH, D, CHUNK = (32, 8, 128, 128)
        ROPE_THETA = 10000.0
        RMS_EPS = 1e-05

        def _rope_tables(L):
            inv_freq = 1.0 / ROPE_THETA ** (jnp.arange(0, D, 2, dtype=jnp.float32) / D)
            ang = jnp.arange(L, dtype=jnp.float32)[:, None] * inv_freq
            cos = jnp.concatenate([jnp.cos(ang), jnp.cos(ang)], axis=-1)[:, None, :]
            sin = jnp.concatenate([jnp.sin(ang), jnp.sin(ang)], axis=-1)[:, None, :]
            return (cos, sin)

        def _apply_rope(x, cos, sin):
            half = D // 2
            rot = jnp.concatenate([-x[..., half:], x[..., :half]], axis=-1)
            return x * cos + rot * sin
        B, L, HID = hidden_states.shape
        NC = L // CHUNK
        q = (hidden_states @ Wq.T).reshape(B, L, H, D)
        k = (hidden_states @ Wk.T).reshape(B, L, KVH, D)
        v = (hidden_states @ Wv.T).reshape(B, L, KVH, D)
        cos, sin = _rope_tables(L)
        q = _apply_rope(q, cos, sin)
        k = _apply_rope(k, cos, sin)
        k = jnp.repeat(k, H // KVH, axis=2)
        v = jnp.repeat(v, H // KVH, axis=2)
        dt = jax.nn.softplus(hidden_states @ Win.T + dt_bias)
        A = -jnp.exp(A_log_bias)
        g = dt * A

        def chunked(t):
            return t.transpose(0, 2, 1, 3).reshape(B, H, NC, CHUNK, D)
        qc, kc = (chunked(q), chunked(k))
        xc = chunked(v * dt[..., None])
        gc = g.transpose(0, 2, 1).reshape(B, H, NC, CHUNK)
        G = jnp.cumsum(gc, axis=-1)
        scores = jnp.einsum('bhnid,bhnjd->bhnij', qc, kc)
        idx = jnp.arange(CHUNK)
        causal = idx[:, None] >= idx[None, :]
        decay = jnp.where(causal, jnp.exp(G[..., :, None] - G[..., None, :]), 0.0)
        y_intra = jnp.einsum('bhnij,bhnjd->bhnid', scores * decay, xc)
        Glast = G[..., -1:]
        k_dec = kc * jnp.exp(Glast - G)[..., None]
        cstates = jnp.einsum('bhnjd,bhnje->bhnde', k_dec, xc)
        chunk_decay = jnp.exp(G[..., -1])

        def step(state, inp):
            dec, cs = inp
            return (state * dec + cs, state)
        init = jnp.zeros((B, H, D, D), hidden_states.dtype)
        _, prev = lax.scan(step, init, (chunk_decay.transpose(2, 0, 1)[..., None, None], cstates.transpose(2, 0, 1, 3, 4)))
        prev = prev.transpose(1, 2, 0, 3, 4)
        y_inter = jnp.einsum('bhnid,bhnde->bhnie', qc * jnp.exp(G)[..., None], prev)
        y = (y_intra + y_inter).reshape(B, H, L, D).transpose(0, 2, 1, 3)
        rms = jnp.sqrt(jnp.mean(jnp.square(y), axis=-1, keepdims=True) + RMS_EPS)
        y = y / rms * gnorm_w
        gate = (hidden_states @ Wg.T).reshape(B, L, H, D)
        y = y * (gate * jax.nn.sigmoid(gate))
        return y.reshape(B, L, H * D) @ Wo.T

    def _L0_xattn_ref(hidden_states, key_value_states, attention_mask, position_bias, ln_weight, w_q, w_k, w_v, w_out):
        import jax, jax.numpy as jnp
        import numpy as np
        B, LQ, LK, D, H, DH = (2, 128, 128, 512, 32, 128)
        EPS = 1e-05

        def _rmsnorm(x, weight):
            var = jnp.mean(jnp.square(x), axis=-1, keepdims=True)
            return x * jax.lax.rsqrt(var + EPS) * weight
        x = _rmsnorm(hidden_states, ln_weight)
        b, lq, _ = x.shape
        lk = key_value_states.shape[1]
        h_q = (x @ w_q.T).reshape(b, lq, H, DH)
        h_k = (key_value_states @ w_k.T).reshape(b, lk, H, DH)
        h_v = (key_value_states @ w_v.T).reshape(b, lk, H, DH)
        score = jnp.einsum('bqhd,bkhd->bhqk', h_q, h_k)
        score = score + position_bias[None]
        m = attention_mask[:, None]
        score = jnp.where(m, score, -jnp.inf)
        score = jax.nn.softmax(score, axis=-1)
        score = jnp.where(m, score, 0.0)
        attn = jnp.einsum('bhqk,bkhd->bqhd', score, h_v).reshape(b, lq, H * DH)
        out = attn @ w_out.T
        return hidden_states + out

    def _L0_ffn_ref(hidden_states, gate_w, w_gate_up, w_down, shared_w_gate_up, shared_w_down):
        import jax, jax.numpy as jnp
        import numpy as np
        HIDDEN = 512
        MOE_INTER = 128
        SHARED_INTER = 512
        NUM_EXPERTS = 16
        TOP_K = 2

        def _moe_forward(x, gate_w, w_gate_up, w_down, shared_w_gate_up, shared_w_down):
            orig_shape = x.shape
            x2 = x.reshape(-1, orig_shape[-1])
            gu_s = x2 @ shared_w_gate_up.T
            g_s, u_s = jnp.split(gu_s, 2, axis=-1)
            shared_out = jax.nn.silu(g_s) * u_s @ shared_w_down.T
            logits = x2 @ gate_w.T
            probs = jax.nn.softmax(logits, axis=-1)
            topk_vals, topk_idx = jax.lax.top_k(probs, TOP_K)
            topk_vals = topk_vals / jnp.sum(topk_vals, axis=-1, keepdims=True)
            combine = jnp.sum(jax.nn.one_hot(topk_idx, NUM_EXPERTS, dtype=x2.dtype) * topk_vals[..., None], axis=1)
            gu = jnp.einsum('th,eih->eti', x2, w_gate_up)
            g, u = jnp.split(gu, 2, axis=-1)
            act = jax.nn.silu(g) * u
            out_e = jnp.einsum('eti,ehi->eth', act, w_down)
            moe_out = jnp.einsum('eth,te->th', out_e, combine)
            return (moe_out + shared_out).reshape(orig_shape)
        return _moe_forward(hidden_states, gate_w, w_gate_up, w_down, shared_w_gate_up, shared_w_down)
    x = x + _L0_attn_ref(_layernorm(x, axis=-1), L0_attn_Wq, L0_attn_Wk, L0_attn_Wv, L0_attn_Wo, L0_attn_Wg, L0_attn_Win, L0_attn_dt_bias, L0_attn_A_log_bias, L0_attn_gnorm_w)
    x = x + _L0_xattn_ref(_layernorm(x, axis=-1), ctx_4096, mask_BxSxS2_bk0, L0_xattn_position_bias, L0_xattn_ln_weight, L0_xattn_w_q, L0_xattn_w_k, L0_xattn_w_v, L0_xattn_w_out)
    x = x + _L0_ffn_ref(_layernorm(x, axis=-1), L0_ffn_gate_w, L0_ffn_w_gate_up, L0_ffn_w_down, L0_ffn_shared_w_gate_up, L0_ffn_shared_w_down)
    return x

_drawn_inputs = setup_inputs


def setup_inputs(seed=0):
    import zlib

    import numpy as np

    out = dict(_drawn_inputs(seed))
    spreads = {'L0_attn_dt_bias': (0.0, 0.8),
     'L0_attn_gnorm_w': (1.0, 0.6),
     'L0_xattn_ln_weight': (1.0, 0.2)}
    factors = {'L0_ffn_gate_w': 7.055,
     'L0_ffn_w_gate_up': 6.548,
     'L0_ffn_w_down': 6.556,
     'L0_ffn_shared_w_gate_up': 8.0,
     'L0_ffn_shared_w_down': 8.0}
    for name, (base, spread) in spreads.items():
        noise = np.random.default_rng([zlib.crc32(name.encode()), seed]).standard_normal(out[name].shape)
        drawn = base * np.exp(spread * noise) if base else spread * noise
        out[name] = jnp.asarray(drawn.astype(out[name].dtype))
    for name, factor in factors.items():
        out[name] = (out[name] * factor).astype(out[name].dtype)
    return out
```

```python
from contextlib import ExitStack

import concourse.bass as bass
from concourse import mybir

F32 = mybir.dt.float32
F32R = mybir.dt.float32r
BF16 = mybir.dt.bfloat16
I32 = mybir.dt.int32
U8 = mybir.dt.uint8
ALU = mybir.AluOpType
ACT = mybir.ActivationFunctionType
AX_X = mybir.AxisListType.X

P = 128
NB = 8
HID = 512
KT = HID // P
HALF = 512
BPH = HALF // P
HPG = 4
NG = 8
NH = NG * HPG
NEXP = 16
NCOMB = NEXP + HPG
NU = NCOMB // HPG
EPS = 1e-5
NEG = -1e30
TILES_QK = 2 * (1 + HPG)
FIRST_TILES = 1 + HPG
STEP_TILES = {0: (5, 6), 1: (7,), 2: (8,), 3: (9,)}
STEP_SPLITS = {4: (0, 1), 5: (2,), 6: (3,)}
RING = 3
NEWTON = 3
RSQRT_MAGIC = 0x5F3759DF
ROUTE_STEPS = 22
COMB_STEPS = ROUTE_STEPS + 10
DT_STEPS = 26 + NB


def later(g, b, lag=1):
    return not isinstance(g, int) or NB * g + b >= lag


def before(g, half):
    return (g, 0) if half else (g - 1, 1)


def per_head(column, width=P):
    return column.unsqueeze(2).broadcast_to([column.shape[0], column.shape[1], width])


def heads(tile):
    return tile.rearrange("p (h d) -> p h d", h=HPG)


def product3(pe, out, left, right, first, last):
    (lh, ll), (rh, rl) = left, right
    pe.matmul(out, lh, rh, start=first, stop=False)
    pe.matmul(out, lh, rl, start=False, stop=False)
    return pe.matmul(out, ll, rh, start=False, stop=last)


class Norm:

    def __init__(self, sb, sem, tag):
        self.st = sb(f"{tag}_stats", [P, NB, 6], F32)
        self.mv = sb(f"{tag}_mean_var", [P, NB, 2], F32)
        self.ve = sb(f"{tag}_var_eps", [P, NB], F32)
        self.sd = sb(f"{tag}_std", [P, NB], F32)
        self.rs = sb(f"{tag}_rstd", [P, NB], F32)
        self.stats_done = sem(f"{tag}_stats_done")
        self.var_ready = sem(f"{tag}_var_ready")
        self.std_ready = sem(f"{tag}_std_ready")
        self.rstd_ready = sem(f"{tag}_rstd_ready")
        self.xn_ready = sem(f"{tag}_xn_ready")
        self.turned = sem(f"{tag}_turned")
        self.high_ready = sem(f"{tag}_high_ready")
        self.low_ready = sem(f"{tag}_low_ready")


def norm_vector_stats(dve, n, x_res):
    for b in range(NB):
        dve.bn_stats(n.st[:, b, :], x_res[:, b, :]).then_inc(n.stats_done, 1)
    dve.wait_ge(n.stats_done, NB)
    for b in range(NB):
        dve.bn_aggr(n.mv[:, b, :], n.st[:, b, :]).then_inc(n.stats_done, 1)
    dve.wait_ge(n.stats_done, 2 * NB)
    dve.tensor_scalar(n.ve[:, :], n.mv[:, :, 1], EPS, None, ALU.add).then_inc(n.var_ready, 1)
    dve.wait_ge(n.std_ready, 1)
    dve.reciprocal(n.rs[:, :], n.sd[:, :]).then_inc(n.rstd_ready, 1)
    dve.wait_ge(n.rstd_ready, 1)


def norm_scalar_std(act, n, count=1):
    act.wait_ge(n.var_ready, count)
    act.activation(n.sd[:, :], n.ve[:, :], ACT.Sqrt).then_inc(n.std_ready, 1)


def norm_tensor_turn(pe, n, xn, ident, banks):
    for b in range(NB):
        pe.wait_ge(n.xn_ready, b + 1)
        if b >= 2:
            pe.wait_ge(n.low_ready, b - 1)
        for k in range(KT):
            mm = pe.transpose(banks[b % 2][:, k * P:(k + 1) * P], xn[:, b, k * P:(k + 1) * P], ident[:, :])
        mm.then_inc(n.turned, 1)


def self_attention(nc, ctx, x_res, act_h, act_l, ident, const, w, x_dram):

    def sb(name, shape, dt):
        return ctx.enter_context(nc.sbuf_tensor(name, shape, dt))

    def sem(name):
        return ctx.enter_context(nc.semaphore(name))

    def psum(name):
        return ctx.enter_context(nc.psum_tensor(name, [P, 512], F32))

    QK = (HPG + 1) * P
    raw_a = sb("raw_a", [P, KT, QK], F32)
    raw_b = sb("raw_b", [P, KT, HALF], F32)
    wqk = [sb(f"wqk_{s}", [P, KT, QK], F32R) for s in ("high", "low")]
    wg = [sb(f"wg_{s}", [P, KT, HALF], F32R) for s in ("high", "low")]
    wo = [sb(f"wo_{s}", [P, HPG, HID], F32R) for s in ("high", "low")]
    gnorm = sb("gnorm", [P, 2], F32)
    cos = sb("cos", [P, P], F32)
    sin = sb("sin", [P, P], F32)
    causal = sb("causal", [P, HPG * P], BF16)
    ident_b = sb("ident_b", [P, P], BF16)
    pick = sb("pick", [3 * NH, NH], BF16)
    cum3 = sb("cum3", [3 * NH, NB * P], BF16)
    bias3 = sb("bias3", [3 * NH, NB * P], BF16)
    v_tok = sb("v_tok", [P, NB, NG * P], F32)
    q_t = sb("q_t", [P, 2, HPG, HALF], F32)
    k_t = sb("k_t", [P, 2, HALF], F32)
    turned_q = sb("turned_q", [P, 2, HALF], F32)
    tanh = sb("tanh", [P, HALF], F32)
    gate = sb("gate", [P, 2, HALF], F32)
    decay = sb("decay", [P, HALF], F32)
    prob = sb("prob", [P, 2, HALF], F32)
    square = sb("square", [P, HALF], F32)
    z = sb("z", [P, 2, HALF], F32)
    zt = [sb(f"zt_{s}", [P, HALF], F32R) for s in ("high", "low")]
    ssq = sb("ssq", [P, 8, HPG], F32)

    proj = [psum(f"ps_proj{i}") for i in range(RING)]
    ps_d, ps_s, ps_y, ps_t, ps_o = (psum(f"ps_{n}") for n in ("decay", "scores", "y", "turn", "out"))

    n = Norm(sb, sem, "self")
    ld_x, ld_c, ld_dt = sem("ld_x"), sem("ld_c"), sem("ld_dt")
    ld_v0, ld_v1, ld_qk, ld_g, ld_o = sem("ld_v0"), sem("ld_v1"), sem("ld_qk"), sem("ld_g"), sem("ld_o")
    zero_ready, const_ready = sem("zero_ready"), sem("const_ready")
    act_wv, dve_wv = sem("act_wv"), sem("dve_wv")
    act_win, dve_win = sem("act_win"), sem("dve_win")
    act_wqk, dve_wqk = sem("act_wqk"), sem("dve_wqk")
    act_wg, dve_wg = sem("act_wg"), sem("dve_wg")
    act_wo, dve_wo = sem("act_wo"), sem("dve_wo")
    pe_dt, dt_step, act_dt = sem("pe_dt"), sem("dt_step"), sem("act_dt")
    pe_v, act_v = sem("pe_v"), sem("act_v")
    pe_qk, pe_g, pe_d, pe_s, pe_y, pe_t, pe_o = (sem(f"pe_{s}") for s in ("qk", "g", "d", "s", "y", "t", "o"))
    dve_cos, act_turn, pool_sin, dve_rope = sem("dve_cos"), sem("act_turn"), sem("pool_sin"), sem("dve_rope")
    act_tanh, dve_gate, act_decay, dve_prob = sem("act_tanh"), sem("dve_gate"), sem("act_decay"), sem("dve_prob")
    act_square, dve_ssq, pool_newton, pool_z = sem("act_square"), sem("dve_ssq"), sem("pool_newton"), sem("pool_z")
    dve_z, act_zt, dve_zt, dve_acc = sem("dve_z"), sem("act_zt"), sem("dve_zt"), sem("dve_acc")

    win_raw = raw_b[:, :, 0:NH]
    win = [wqk[s][:, :, 0:P] for s in (0, 1)]

    def rows(i):
        return q_t[0:NH, i // 2, 2 * (i % 2):2 * (i % 2) + 2, :].rearrange("p a n -> p (a n)")

    z_row, e_row, dt_row, cum_row = rows(0), rows(1), rows(2), rows(3)
    k_rows = k_t[0:NH, :, :].rearrange("p a n -> p (a n)")
    t_rows = turned_q[0:NH, :, :].rearrange("p a n -> p (a n)")
    piece = prob[0:NH, 0, :].bitcast(BF16)
    head_col = sb("head_col", [NH, 4], F32)
    xn = v_tok[:, :, 0:HID]

    order = [("qk", t) for t in range(FIRST_TILES)]
    for step in range(NB):
        order += [("gate", step)] + [("qk", t) for t in STEP_TILES.get(step, ())]

    def ring_bank(kind, i):
        return proj[order.index((kind, i)) % RING]

    block = ctx.enter_context(nc.Block())

    @block.sync
    def _(sp):
        for b in range(0, NB, 2):
            sp.dma_start(x_res[:, b:b + 2, :], x_dram[b:b + 2].rearrange("b p d -> p b d")).then_inc(ld_x, 16)
        sp.dma_start(ident[:, :], const["ident"]).then_inc(ld_c, 16)
        sp.dma_start(cos[:, :], const["cos"]).then_inc(ld_c, 16)
        sp.dma_start(sin[:, :], const["sin"]).then_inc(ld_c, 16)
        sp.dma_start(decay[:, :], const["causal"]).then_inc(ld_c, 16)
        sp.dma_start(square[0:3 * NH, 0:NH], const["pick"]).then_inc(ld_c, 16)
        sp.dma_start(gnorm[:, 0:1], w["gnorm"]).then_inc(ld_c, 16)
        sp.dma_start(head_col[:, 0:1], w["dt_bias"]).then_inc(ld_c, 16)
        sp.dma_start(head_col[:, 1:2], w["A_log"]).then_inc(ld_c, 16)
        sp.dma_start(win_raw, w["Win"]).then_inc(ld_dt, 16)
        sp.dma_start(raw_a[:, :, 0:HALF], w["Wv"][0]).then_inc(ld_v0, 16)
        sp.wait_ge(dve_win, KT)
        sp.dma_start(raw_b[:, :, :], w["Wv"][1]).then_inc(ld_v1, 16)
        sp.wait_ge(dve_wv, KT)
        sp.dma_start(raw_a[:, :, :], w["Wqk"][0]).then_inc(ld_qk, 16)
        sp.wait_ge(dve_wv, 2 * KT)
        sp.dma_start(raw_b[:, :, :], w["Wg"][0]).then_inc(ld_g, 16)

        def group(g, last):
            sp.wait_ge(dve_wqk, KT * g + KT)
            sp.dma_start(raw_a[:, :, 0:HALF], w["Wo"][bass.ds(g, 1)].rearrange("g p k n -> p (g k) n")).then_inc(ld_o, 16)
            if not last:
                sp.wait_ge(dve_wg, KT * g + KT)
                sp.dma_start(raw_b[:, :, :], w["Wg"][bass.ds(g + 1, 1)].rearrange("g p k n -> p (g k) n")).then_inc(ld_g, 16)
                sp.wait_ge(dve_wo, KT * g + KT)
                sp.dma_start(raw_a[:, :, :], w["Wqk"][bass.ds(g + 1, 1)].rearrange("g p k n -> p (g k) n")).then_inc(ld_qk, 16)

        with sp.Fori(0, NG - 1) as g:
            group(g, False)
        group(NG - 1, True)

    @block.gpsimd
    def _(pool):
        def sine(g, t):
            pool.wait_ge(act_turn, TILES_QK * g + t + 1)
            tile = turned_q[:, t % 2, :].rearrange("p (b s) -> p b s", b=BPH)
            pool.tensor_tensor(tile, tile, sin[:, :].unsqueeze(1).broadcast_to([P, BPH, P]),
                               ALU.mult).then_inc(pool_sin, 1)

        def normalise_z(g, b):
            s = NB * g + b
            guess, t, minus_half, three_halves = (ssq[:, i, :] for i in (3, 4, 5, 6))
            pool.wait_ge(dve_ssq, 5 * s + 5)
            for i in range(NEWTON):
                step = 4 * NEWTON * s + 4 * i
                pool.tensor_tensor(t, guess, guess, ALU.mult).then_inc(pool_newton, 1)
                pool.wait_ge(pool_newton, step + 1)
                pool.tensor_tensor(t, t, minus_half, ALU.mult).then_inc(pool_newton, 1)
                pool.wait_ge(pool_newton, step + 2)
                pool.tensor_tensor(t, t, three_halves, ALU.add).then_inc(pool_newton, 1)
                pool.wait_ge(pool_newton, step + 3)
                pool.tensor_tensor(guess, guess, t, ALU.mult).then_inc(pool_newton, 1)
                pool.wait_ge(pool_newton, step + 4)
            pool.wait_ge(dve_z, s + 1)
            pool.tensor_tensor(heads(z[:, b % 2, :]), heads(z[:, b % 2, :]), per_head(guess),
                               ALU.mult).then_inc(pool_z, 1)

        def group(g, first):
            for t in range(FIRST_TILES):
                sine(g, t)
                if t == 1 and not first:
                    normalise_z(g - 1, NB - 1)
            for b in range(NB):
                for t in STEP_TILES.get(b, ()):
                    sine(g, t)
                if b >= 1:
                    normalise_z(g, b - 1)

        pool.memset(ssq[:, 6, :], 1.5).then_inc(zero_ready, 1)
        for part in win:
            pool.memset(part[:, :, NH:P].bitcast(F32), 0.0).then_inc(zero_ready, 1)
        pool.wait_ge(ld_c, 16 * 8)
        pool.wait_ge(zero_ready, 3)
        group(0, True)
        with pool.Fori(1, NG) as g:
            group(g, False)
        normalise_z(NG - 1, NB - 1)

    @block.scalar
    def _(act):
        norm_scalar_std(act, n)
        act.wait_ge(ld_dt, 16)
        for k in range(KT):
            act.activation(win[0][:, k, 0:NH], win_raw[:, k, :], ACT.Copy).then_inc(act_win, 1)
        act.wait_ge(ld_v0, 16)
        for k in range(KT):
            act.activation(wg[0][:, k, :], raw_a[:, k, 0:HALF], ACT.Copy).then_inc(act_wv, 1)
        act.wait_ge(ld_v1, 16)
        for k in range(KT):
            act.activation(wo[0][:, k, :], raw_b[:, k, :], ACT.Copy).then_inc(act_wv, 1)
        for b in range(NB):
            act.wait_ge(n.turned, b + 1)
            act.activation(act_h[:, :, b * P:(b + 1) * P], heads([ps_t, ps_o][b % 2][:, :]),
                           ACT.Copy).then_inc(n.high_ready, 1)

        def evacuate_v(i):
            act.wait_ge(pe_v, i + 1)
            act.activation(v_tok[:, i // 2, (i % 2) * HALF:(i % 2 + 1) * HALF], proj[i % RING][:, :],
                           ACT.Copy).then_inc(act_v, 1)

        act.wait_ge(ld_c, 16 * 8)
        act.activation(head_col[:, 2:3], head_col[:, 1:2], ACT.Exp).then_inc(act_dt, 1)
        act.wait_ge(dt_step, 4)
        act.activation(e_row, e_row, ACT.Exp).then_inc(act_dt, 1)
        act.wait_ge(act_dt, 2)
        act.activation(e_row, e_row, ACT.Ln, bias=1.0).then_inc(act_dt, 1)
        act.wait_ge(dt_step, 7)
        act.activation(t_rows, k_rows, ACT.Ln).then_inc(act_dt, 1)
        for i in range(2 * NB):
            evacuate_v(i)

        def split_qk(g, k, first):
            if k == 0:
                act.wait_ge(ld_qk, 16 * g + 16)
                if first:
                    act.wait_ge(pe_dt, 2)
                else:
                    act.wait_ge(pe_qk, TILES_QK * g)
            act.activation(wqk[0][:, k, :], raw_a[:, k, :], ACT.Copy).then_inc(act_wqk, 1)

        def split_g(g, k, first):
            if k == 0:
                act.wait_ge(ld_g, 16 * g + 16)
                if first:
                    act.wait_ge(pe_v, 2 * NB)
                else:
                    act.wait_ge(pe_g, NB * g)
            act.activation(wg[0][:, k, :], raw_b[:, k, :], ACT.Copy).then_inc(act_wg, 1)

        def split_o(g, k, first):
            if k == 0:
                act.wait_ge(ld_o, 16 * g + 16)
                if first:
                    act.wait_ge(pe_v, 2 * NB)
                else:
                    act.wait_ge(pe_o, NB * g)
            act.activation(wo[0][:, k, :], raw_a[:, k, 0:HALF], ACT.Copy, scale=gnorm[:, 1:2]).then_inc(act_wo, 1)

        def turn(g, t, first):
            act.wait_ge(dve_cos, TILES_QK * g + t + 1)
            if t >= 2 or not first:
                act.wait_ge(dve_rope, TILES_QK * g + t - 1)
            src = ring_bank("qk", t)
            act.activation(turned_q[0:64, t % 2, :], src[64:128, :], ACT.Copy)
            act.activation(turned_q[64:128, t % 2, :], src[0:64, :], ACT.Copy).then_inc(act_turn, 1)

        def square_y(g, b):
            s = NB * g + b
            act.wait_ge(pe_y, s + 1)
            if later(g, b):
                act.wait_ge(dve_ssq, 5 * s - 4)
            act.activation(square[:, :], ps_y[:, :], ACT.Square).then_inc(act_square, 1)

        def high_z(g, b):
            s = NB * g + b
            act.wait_ge(pe_t, s + 1)
            if later(g, b):
                act.wait_ge(pe_o, s)
            act.activation(zt[0][:, :], ps_t[:, :], ACT.Copy).then_inc(act_zt, 1)

        def gate_tanh(g, b):
            s = NB * g + b
            act.wait_ge(pe_g, s + 1)
            if later(g, b):
                act.wait_ge(dve_gate, s)
            act.activation(tanh[:, :], ring_bank("gate", b)[:, :], ACT.Tanh, scale=0.5).then_inc(act_tanh, 1)

        def exp_decay(g, b):
            s = NB * g + b
            act.wait_ge(pe_d, s + 1)
            if later(g, b):
                act.wait_ge(dve_prob, s)
            act.activation(decay[:, :], ps_d[:, :], ACT.Exp).then_inc(act_decay, 1)

        def group(g, first, last):
            for t in range(FIRST_TILES):
                if t == 0 and not first:
                    high_z(g - 1, NB - 3)
                turn(g, t, first)
                if t < KT:
                    split_g(g, t, first)
                if t == 1 and not first:
                    square_y(g - 1, NB - 1)
                    high_z(g - 1, NB - 2)
                if t == 4 and not first:
                    high_z(g - 1, NB - 1)
            for b in range(NB):
                if b >= 3:
                    high_z(g, b - 3)
                gate_tanh(g, b)
                exp_decay(g, b)
                if b >= 1:
                    square_y(g, b - 1)
                for t in STEP_TILES.get(b, ()):
                    turn(g, t, first)
                if b in (1, 2):
                    split_o(g, 2 * b - 2, first)
                    split_o(g, 2 * b - 1, first)
                if not last:
                    for k in STEP_SPLITS.get(b, ()):
                        split_qk(g + 1, k, False)

        for k in range(KT):
            split_qk(0, k, True)
        group(0, True, False)
        with act.Fori(1, NG - 1) as g:
            group(g, False, False)
        group(NG - 1, False, True)
        high_z(NG - 1, NB - 3)
        square_y(NG - 1, NB - 1)
        high_z(NG - 1, NB - 2)
        high_z(NG - 1, NB - 1)

    @block.vector
    def _(dve):
        dve.wait_ge(ld_x, 16 * NB // 2)
        norm_vector_stats(dve, n, x_res)
        for b in range(NB):
            dve.tensor_scalar(xn[:, b, :], x_res[:, b, :], n.mv[:, b, 0:1], n.rs[:, b:b + 1],
                              ALU.subtract, ALU.mult).then_inc(n.xn_ready, 1)
        for k in range(KT):
            dve.wait_ge(act_win, k + 1)
            dve.tensor_tensor(win[1][:, k, 0:NH], win_raw[:, k, :], win[0][:, k, 0:NH].bitcast(F32),
                              ALU.subtract).then_inc(dve_win, 1)
        dve.wait_ge(ld_c, 16 * 8)
        dve.tensor_copy(causal[:, :], decay[:, :]).then_inc(const_ready, 1)
        dve.tensor_copy(ident_b[:, :], ident[:, :]).then_inc(const_ready, 1)
        dve.tensor_copy(pick[:, :], square[0:3 * NH, 0:NH]).then_inc(const_ready, 1)
        dve.tensor_scalar(gnorm[:, 1:2], gnorm[:, 0:1], 0.5, None, ALU.mult).then_inc(const_ready, 1)
        for k in range(KT):
            dve.wait_ge(act_wv, k + 1)
            dve.tensor_tensor(wg[1][:, k, :], raw_a[:, k, 0:HALF], wg[0][:, k, :].bitcast(F32),
                              ALU.subtract).then_inc(dve_wv, 1)
        for b in range(NB):
            dve.wait_ge(n.high_ready, b + 1)
            cols = slice(b * P, (b + 1) * P)
            dve.tensor_tensor(act_l[:, :, cols], heads([ps_t, ps_o][b % 2][:, :]),
                              act_h[:, :, cols].bitcast(F32), ALU.subtract).then_inc(n.low_ready, 1)
            if b == NB // 2 - 1:
                for k in range(KT):
                    dve.wait_ge(act_wv, KT + k + 1)
                    dve.tensor_tensor(wo[1][:, k, :], raw_b[:, k, :], wo[0][:, k, :].bitcast(F32),
                                      ALU.subtract).then_inc(dve_wv, 1)

        dve.wait_ge(pe_dt, 2)
        for half, bank in enumerate((ps_s, ps_y)):
            dve.tensor_scalar(z_row[:, half * HALF:(half + 1) * HALF], bank[0:NH, :], head_col[:, 0:1], None,
                              ALU.add).then_inc(dt_step, 1)
        dve.wait_ge(dt_step, 2)
        dve.scalar_tensor_tensor(out=e_row, in0=z_row, scalar=-1.0, in1=z_row, op0=ALU.mult,
                                 op1=ALU.min).then_inc(dt_step, 1)
        dve.tensor_scalar(dt_row, z_row, 0.0, None, ALU.max).then_inc(dt_step, 1)
        dve.wait_ge(dt_step, 4)
        dve.wait_ge(act_dt, 3)
        dve.tensor_tensor(dt_row, dt_row, e_row, ALU.add).then_inc(dt_step, 1)
        dve.tensor_scalar(head_col[:, 3:4], head_col[:, 2:3], -1.0, None, ALU.mult).then_inc(dt_step, 1)
        dve.wait_ge(dt_step, 6)
        dve.tensor_scalar(k_rows, dt_row, 1e-37, None, ALU.max).then_inc(dt_step, 1)
        dve.tensor_scalar(z_row, dt_row, head_col[:, 3:4], None, ALU.mult).then_inc(dt_step, 1)
        dve.memset(e_row, 1.0).then_inc(dt_step, 1)
        dve.wait_ge(dt_step, 9)
        for b in range(NB):
            dve.tensor_tensor_scan(cum_row[:, b * P:(b + 1) * P], e_row[:, b * P:(b + 1) * P],
                                   z_row[:, b * P:(b + 1) * P], 0.0, ALU.mult, ALU.add).then_inc(dt_step, 1)
        dve.wait_ge(dt_step, 9 + NB)
        dve.wait_ge(act_dt, 4)
        dve.tensor_tensor(dt_row, t_rows, cum_row, ALU.subtract).then_inc(dt_step, 1)
        count = 10 + NB
        for dst, src in ((cum3, cum_row), (bias3, dt_row)):
            for i in range(3):
                dve.wait_ge(dt_step, count)
                dve.tensor_copy(piece, src).then_inc(dt_step, 1)
                count += 1
                dve.wait_ge(dt_step, count)
                dve.tensor_copy(dst[i * NH:(i + 1) * NH, :], piece).then_inc(dt_step, 1)
                count += 1
                if i < 2:
                    dve.tensor_tensor(src, src, piece, ALU.subtract).then_inc(dt_step, 1)
                    count += 1
        assert count == DT_STEPS

        def low_qk(g, k):
            dve.wait_ge(act_wqk, KT * g + k + 1)
            dve.tensor_tensor(wqk[1][:, k, :], raw_a[:, k, :], wqk[0][:, k, :].bitcast(F32),
                              ALU.subtract).then_inc(dve_wqk, 1)

        def low_g(g, k):
            dve.wait_ge(act_wg, KT * g + k + 1)
            dve.tensor_tensor(wg[1][:, k, :], raw_b[:, k, :], wg[0][:, k, :].bitcast(F32),
                              ALU.subtract).then_inc(dve_wg, 1)

        def low_o(g, k):
            dve.wait_ge(act_wo, KT * g + k + 1)
            dve.scalar_tensor_tensor(out=wo[1][:, k, :], in0=raw_a[:, k, 0:HALF], scalar=gnorm[:, 1:2],
                                     in1=wo[0][:, k, :].bitcast(F32), op0=ALU.mult,
                                     op1=ALU.subtract).then_inc(dve_wo, 1)

        def rope_tile(t):
            half, j = t // FIRST_TILES, t % FIRST_TILES
            return (k_t[:, half, :] if j == 0 else q_t[:, half, j - 1, :]).rearrange("p (b s) -> p b s", b=BPH)

        def cosine(g, t, first):
            dve.wait_ge(pe_qk, TILES_QK * g + t + 1)
            if not first:
                if t == 0:
                    dve.wait_ge(pe_s, NB * g - BPH)
                if t == FIRST_TILES:
                    dve.wait_ge(pe_s, NB * g)
            dve.tensor_tensor(rope_tile(t), ring_bank("qk", t)[:, :].rearrange("p (b s) -> p b s", b=BPH),
                              cos[:, :].unsqueeze(1).broadcast_to([P, BPH, P]), ALU.mult).then_inc(dve_cos, 1)

        def add_sine(g, t):
            dve.wait_ge(pool_sin, TILES_QK * g + t + 1)
            dve.wait_ge(dve_cos, TILES_QK * g + t + 1)
            dve.tensor_tensor(rope_tile(t), rope_tile(t),
                              turned_q[:, t % 2, :].rearrange("p (b s) -> p b s", b=BPH),
                              ALU.add).then_inc(dve_rope, 1)

        def gate_silu(g, b):
            s = NB * g + b
            dve.wait_ge(act_tanh, s + 1)
            if later(g, b, 2):
                dve.wait_ge(dve_z, s - 1)
            dve.scalar_tensor_tensor(out=gate[:, b % 2, :], in0=tanh[:, :], scalar=1.0,
                                     in1=ring_bank("gate", b)[:, :], op0=ALU.add,
                                     op1=ALU.mult).then_inc(dve_gate, 1)

        def decayed(g, b):
            s = NB * g + b
            dve.wait_ge(act_decay, s + 1)
            dve.wait_ge(pe_s, s + 1)
            if later(g, b, 2):
                dve.wait_ge(pe_y, s - 1)
            dve.tensor_tensor(prob[:, b % 2, :], ps_s[:, :], decay[:, :], ALU.mult).then_inc(dve_prob, 1)

        def mean_square(g, b):
            s = NB * g + b
            total, mean, shifted, guess, minus_half = (ssq[:, i, :] for i in (0, 1, 2, 3, 5))
            dve.wait_ge(act_square, s + 1)
            dve.tensor_reduce(total, heads(square[:, :]), AX_X, ALU.add).then_inc(dve_ssq, 1)
            dve.wait_ge(dve_ssq, 5 * s + 1)
            if later(g, b):
                dve.wait_ge(pool_z, s)
            dve.tensor_scalar(mean, total, 1.0 / P, EPS, ALU.mult, ALU.add).then_inc(dve_ssq, 1)
            dve.tensor_scalar(minus_half, total, -0.5 / P, -0.5 * EPS, ALU.mult, ALU.add).then_inc(dve_ssq, 1)
            dve.wait_ge(dve_ssq, 5 * s + 2)
            dve.tensor_scalar(shifted.bitcast(I32), mean.bitcast(I32), 1, None,
                              ALU.logical_shift_right).then_inc(dve_ssq, 1)
            dve.wait_ge(dve_ssq, 5 * s + 4)
            dve.tensor_scalar(guess.bitcast(I32), shifted.bitcast(I32), -1, RSQRT_MAGIC, ALU.mult,
                              ALU.add).then_inc(dve_ssq, 1)

        def gated(g, b):
            s = NB * g + b
            dve.wait_ge(act_square, s + 1)
            if later(g, b, 2):
                dve.wait_ge(pe_t, s - 1)
            dve.tensor_tensor(z[:, b % 2, :], ps_y[:, :], gate[:, b % 2, :], ALU.mult).then_inc(dve_z, 1)

        def low_z(g, b):
            s = NB * g + b
            dve.wait_ge(act_zt, s + 1)
            dve.tensor_tensor(zt[1][:, :], ps_t[:, :], zt[0][:, :].bitcast(F32), ALU.subtract).then_inc(dve_zt, 1)

        def accumulate(g, b):
            s = NB * g + b
            dve.wait_ge(pe_o, s + 1)
            if later(g, b):
                dve.wait_ge(dve_acc, s)
            dve.tensor_tensor(x_res[:, b, :], x_res[:, b, :], ps_o[:, :], ALU.add).then_inc(dve_acc, 1)

        def group(g, first, last):
            for t in range(FIRST_TILES):
                if t == 0 and not first:
                    low_z(g - 1, NB - 3)
                cosine(g, t, first)
                if t >= 1:
                    add_sine(g, t - 1)
                if t < KT:
                    low_g(g, t)
                if not first:
                    if t == 1:
                        accumulate(g - 1, NB - 3)
                        gated(g - 1, NB - 1)
                        mean_square(g - 1, NB - 1)
                        low_z(g - 1, NB - 2)
                    if t == 4:
                        accumulate(g - 1, NB - 2)
            add_sine(g, FIRST_TILES - 1)
            if not first:
                low_z(g - 1, NB - 1)
            for b in range(NB):
                tiles = STEP_TILES.get(b, ())
                if b >= 3:
                    low_z(g, b - 3)
                gate_silu(g, b)
                decayed(g, b)
                if b >= 1:
                    gated(g, b - 1)
                    mean_square(g, b - 1)
                for t in tiles:
                    cosine(g, t, first)
                    if t != tiles[0]:
                        add_sine(g, t - 1)
                if b == 0 and not first:
                    accumulate(g - 1, NB - 1)
                if b in (1, 2):
                    low_o(g, 2 * b - 2)
                    low_o(g, 2 * b - 1)
                if b >= 3:
                    accumulate(g, b - 3)
                if not last:
                    for k in STEP_SPLITS.get(b, ()):
                        low_qk(g + 1, k)
                if tiles:
                    add_sine(g, tiles[-1])

        for k in range(KT):
            low_qk(0, k)
        group(0, True, False)
        with dve.Fori(1, NG - 1) as g:
            group(g, False, False)
        group(NG - 1, False, True)
        low_z(NG - 1, NB - 3)
        gated(NG - 1, NB - 1)
        mean_square(NG - 1, NB - 1)
        accumulate(NG - 1, NB - 3)
        low_z(NG - 1, NB - 2)
        accumulate(NG - 1, NB - 2)
        low_z(NG - 1, NB - 1)
        accumulate(NG - 1, NB - 1)

    @block.tensor
    def _(pe):
        pe.wait_ge(ld_c, 16 * 8)
        norm_tensor_turn(pe, n, xn, ident, [ps_t, ps_o])
        pe.wait_ge(n.low_ready, NB)
        pe.wait_ge(n.high_ready, NB)
        pe.wait_ge(dve_win, KT)
        pe.wait_ge(zero_ready, 3)
        for half, bank in enumerate((ps_s, ps_y)):
            toks = slice(half * HALF, (half + 1) * HALF)
            for k in range(KT):
                mm = product3(pe, bank[:, :], [s[:, k, :] for s in win], (act_h[:, k, toks], act_l[:, k, toks]),
                              k == 0, k == KT - 1)
            mm.then_inc(pe_dt, 1)
        for i in range(2 * NB):
            b, part = i // 2, i % 2
            pe.wait_ge(dve_wv, KT * (part + 1))
            if i >= RING:
                pe.wait_ge(act_v, i - RING + 1)
            for k in range(KT):
                wv = (wg, wo)[part]
                mm = product3(pe, proj[i % RING][:, :],
                              (act_h[:, k, b * P:(b + 1) * P], act_l[:, k, b * P:(b + 1) * P]),
                              (wv[0][:, k, :], wv[1][:, k, :]), k == 0, k == KT - 1)
            mm.then_inc(pe_v, 1)

        def bank_free(g, kind, i, first):
            place = order.index((kind, i)) - RING
            if place < 0:
                if first:
                    return
                g = g - 1
            kind, i = order[place]
            if kind == "qk":
                pe.wait_ge(act_turn, TILES_QK * g + i + 1)
            else:
                pe.wait_ge(dve_gate, NB * g + i + 1)

        def qk_tile(g, t, first):
            half, j = t // FIRST_TILES, t % FIRST_TILES
            toks = slice(half * HALF, (half + 1) * HALF)
            if t == 0:
                pe.wait_ge(dve_wqk, KT * g + KT)
            bank_free(g, "qk", t, first)
            cols = slice(j * P, (j + 1) * P)
            for k in range(KT):
                mm = product3(pe, ring_bank("qk", t)[:, :], (wqk[0][:, k, cols], wqk[1][:, k, cols]),
                              (act_h[:, k, toks], act_l[:, k, toks]), k == 0, k == KT - 1)
            mm.then_inc(pe_qk, 1)

        def gate_tile(g, b):
            if b == 0:
                pe.wait_ge(dve_wg, KT * g + KT)
            bank_free(g, "gate", b, False)
            toks = slice(b * P, (b + 1) * P)
            for k in range(KT):
                mm = product3(pe, ring_bank("gate", b)[:, :], (act_h[:, k, toks], act_l[:, k, toks]),
                              (wg[0][:, k, :], wg[1][:, k, :]), k == 0, k == KT - 1)
            mm.then_inc(pe_g, 1)

        def decay_logs(g, b):
            s = NB * g + b
            if later(g, b):
                pe.wait_ge(act_decay, s)
            toks = slice(b * P, (b + 1) * P)
            pe.matmul(ps_d[:, :], ident_b[:, :], causal[:, :], start=True, stop=False, skip_group_check=True)
            pe.matmul(ps_d[:, :], bias3[:, toks],
                      pick[:, bass.ds(g * HPG, HPG)].unsqueeze(2).broadcast_to([3 * NH, HPG, P]),
                      start=False, stop=False, skip_group_check=True)
            for h in range(HPG):
                mm = pe.matmul(ps_d[:, h * P:(h + 1) * P],
                               pick[:, bass.ds(g * HPG + h, 1)].broadcast_to([3 * NH, P]), cum3[:, toks],
                               start=False, stop=h == HPG - 1, skip_group_check=True)
            mm.then_inc(pe_d, 1)

        def scores(g, b):
            s = NB * g + b
            if b % BPH == 0:
                pe.wait_ge(dve_rope, TILES_QK * g + (b // BPH + 1) * FIRST_TILES)
            if later(g, b):
                pe.wait_ge(dve_prob, s)
            half, toks = b // BPH, slice((b % BPH) * P, (b % BPH + 1) * P)
            pe.matmul(ps_s[:, :], k_t[:, half, toks], q_t[:, half, :, toks], start=True, stop=True).then_inc(pe_s, 1)

        def out_y(g, b):
            s = NB * g + b
            pe.wait_ge(dve_prob, s + 1)
            if later(g, b):
                pe.wait_ge(dve_z, s)
            for h in range(HPG):
                mm = pe.matmul(ps_y[:, h * P:(h + 1) * P], prob[:, b % 2, h * P:(h + 1) * P],
                               v_tok[:, b, bass.ds(g * P, P)], start=True, stop=True)
            mm.then_inc(pe_y, 1)

        def turn_z(g, b):
            s = NB * g + b
            pe.wait_ge(pool_z, s + 1)
            if later(g, b):
                pe.wait_ge(dve_zt, s)
            for h in range(HPG):
                mm = pe.transpose(ps_t[:, h * P:(h + 1) * P], z[:, b % 2, h * P:(h + 1) * P], ident[:, :])
            mm.then_inc(pe_t, 1)

        def project(g, b):
            s = NB * g + b
            if b == 0:
                pe.wait_ge(dve_wo, KT * g + KT)
            pe.wait_ge(dve_zt, s + 1)
            if later(g, b):
                pe.wait_ge(dve_acc, s)
            for h in range(HPG):
                cols = slice(h * P, (h + 1) * P)
                mm = product3(pe, ps_o[:, :], (zt[0][:, cols], zt[1][:, cols]), (wo[0][:, h, :], wo[1][:, h, :]),
                              h == 0, h == HPG - 1)
            mm.then_inc(pe_o, 1)

        def group(g, first):
            for t in range(FIRST_TILES):
                qk_tile(g, t, first)
                if t == 1 and not first:
                    project(g - 1, NB - 3)
                    out_y(g - 1, NB - 1)
                    turn_z(g - 1, NB - 2)
                if t == 4 and not first:
                    project(g - 1, NB - 2)
                    turn_z(g - 1, NB - 1)
            for b in range(NB):
                gate_tile(g, b)
                decay_logs(g, b)
                scores(g, b)
                if b >= 1:
                    out_y(g, b - 1)
                for t in STEP_TILES.get(b, ()):
                    qk_tile(g, t, first)
                if b == 0 and not first:
                    project(g - 1, NB - 1)
                if b >= 3:
                    project(g, b - 3)
                if b >= 2:
                    turn_z(g, b - 2)

        pe.wait_ge(act_v, 2 * NB)
        pe.wait_ge(const_ready, 4)
        pe.wait_ge(dt_step, DT_STEPS)
        group(0, True)
        with pe.Fori(1, NG) as g:
            group(g, False)
        project(NG - 1, NB - 3)
        out_y(NG - 1, NB - 1)
        turn_z(NG - 1, NB - 2)
        project(NG - 1, NB - 2)
        turn_z(NG - 1, NB - 1)
        project(NG - 1, NB - 1)


def cross_attention(nc, ctx, x_res, act_h, act_l, ident, const, w, context, mask):

    def sb(name, shape, dt):
        return ctx.enter_context(nc.sbuf_tensor(f"x_{name}", shape, dt))

    def sem(name):
        return ctx.enter_context(nc.semaphore(f"x_{name}"))

    def psum(name):
        return ctx.enter_context(nc.psum_tensor(f"x_ps_{name}", [P, 512], F32))

    raw_a = sb("raw_a", [P, KT, HALF], F32)
    raw_b = sb("raw_b", [P, KT, HALF], F32)
    wk, wq, wv, wo = ([sb(f"w{m}_{s}", [P, KT, HALF], F32R) for s in ("high", "low")] for m in "kqvo")
    ctx_h = sb("ctx_high", [P, KT, NB * P], F32R)
    ctx_l = sb("ctx_low", [P, KT, NB * P], F32R)
    ln_w = sb("ln_w", [P, KT], F32)
    ident_b = sb("ident_b", [P, P], BF16)
    mask_words = sb("mask_words", [P, NB, P // 4], I32)
    bar = sb("bar", [P, NB, P], BF16)
    pos = sb("pos", [P, HPG, P], F32)
    kqv = sb("kqv", [P, 3 * HPG, HALF], F32)
    k_t, q_t, v_tok = (kqv[:, i * HPG:(i + 1) * HPG, :] for i in range(3))
    h_tok = kqv[:, 0:NB, :]
    score = sb("score", [P, 3, HALF], F32)
    prob_t = sb("prob_t", [P, HALF], F32)
    at = [sb(f"at_{s}", [P, HALF], F32R) for s in ("high", "low")]
    top, total, inverse = (sb(name, [P, HPG], F32) for name in ("top", "total", "inverse"))
    neg_top, row_sum = (sb(name, [P, 2, HPG], F32) for name in ("neg_top", "row_sum"))
    ssq = sb("ssq", [P, 4, NB], F32)

    proj = [psum(f"proj{i}") for i in range(RING)]
    ps_s, ps_t, ps_y, ps_o = (psum(s) for s in ("scores", "turn", "y", "out"))

    n = Norm(sb, sem, "ln")
    ld_c, ld_mask, ld_ctx0, ld_ctx1 = sem("ld_c"), sem("ld_mask"), sem("ld_ctx0"), sem("ld_ctx1")
    ld = {m: sem(f"ld_w{m}") for m in "kqvo"}
    ld_pos = sem("ld_pos")
    act_w = {m: sem(f"act_w{m}") for m in "kqvo"}
    dve_w = {m: sem(f"dve_w{m}") for m in "kqvo"}
    weights = dict(k=wk, q=wq, v=wv, o=wo)
    raw = dict(k=raw_a, v=raw_a, q=raw_b, o=raw_b)
    act_ctx, dve_ctx, const_ready = sem("act_ctx"), sem("dve_ctx"), sem("const_ready")
    h_ready, act_hsq, rms_step, rms_std = sem("h_ready"), sem("act_hsq"), sem("rms_step"), sem("rms_std")
    pe_pr, act_pr = sem("pe_pr"), sem("act_pr")
    pe_s, pe_t, pe_y, pe_o = sem("pe_s"), sem("pe_t"), sem("pe_y"), sem("pe_o")
    dve_sum, dve_max, act_exp, dve_inv = sem("dve_sum"), sem("dve_max"), sem("act_exp"), sem("dve_inv")
    pool_norm, dve_pt, act_at, dve_at, dve_acc = (sem("pool_norm"), sem("dve_pt"), sem("act_at"), sem("dve_at"),
                                                  sem("dve_acc"))
    TILES = 2 * HPG
    PER = TILES + BPH
    DRAIN = 4

    def parts(k):
        return [k - lag if 0 <= k - lag < BPH else None for lag in range(5)]

    def any_later(g, half, b, lag=1):
        return later(g, BPH * half + b, lag)

    block = ctx.enter_context(nc.Block())

    @block.sync
    def _(sp):
        sp.dma_start(raw_a[:, :, :], context[0]).then_inc(ld_ctx0, 16)
        sp.dma_start(raw_b[:, :, :], context[1]).then_inc(ld_ctx1, 16)
        sp.dma_start(ln_w[:, :], w["ln_w"]).then_inc(ld_c, 16)
        sp.dma_start(mask_words[:, :, :], mask).then_inc(ld_mask, 16)
        sp.dma_start(pos[:, :, :], w["pos"][0]).then_inc(ld_pos, 16)
        sp.wait_ge(dve_ctx, KT)
        sp.dma_start(raw_a[:, :, :], w["Xk"][0]).then_inc(ld["k"], 16)
        sp.wait_ge(dve_ctx, 2 * KT)
        sp.dma_start(raw_b[:, :, :], w["Xq"][0]).then_inc(ld["q"], 16)

        def load(m, g):
            sp.dma_start(raw[m][:, :, :], w[f"X{m}"][bass.ds(g, 1)].rearrange("g p k n -> p (g k) n")).then_inc(ld[m], 16)

        def group(g, last):
            sp.wait_ge(dve_w["k"], KT * g + KT)
            load("v", g)
            sp.wait_ge(dve_w["q"], KT * g + KT)
            load("o", g)
            if not last:
                sp.wait_ge(dve_w["v"], KT * g + KT)
                load("k", g + 1)
                sp.wait_ge(dve_w["o"], KT * g + KT)
                load("q", g + 1)
                sp.wait_ge(dve_sum, NB * g + NB)
                sp.dma_start(pos[:, :, :], w["pos"][bass.ds(g + 1, 1)].rearrange("g q h k -> q (g h) k")).then_inc(ld_pos, 16)

        with sp.Fori(0, NG - 1) as g:
            group(g, False)
        group(NG - 1, True)

    @block.gpsimd
    def _(pool):
        def normalise(g, b):
            s = NB * g + b
            pool.wait_ge(dve_inv, 2 * s + 2)
            tile = heads(score[:, b % BPH % 3, :])
            pool.tensor_tensor(tile, tile, per_head(inverse[:, :]), ALU.mult).then_inc(pool_norm, 1)

        with pool.Fori(0, NG) as g:
            for b in range(NB):
                normalise(g, b)

    @block.scalar
    def _(act):
        act.wait_ge(ld_ctx0, 16)
        for k in range(KT):
            act.activation(ctx_h[:, k, 0:HALF], raw_a[:, k, :], ACT.Copy).then_inc(act_ctx, 1)
        norm_scalar_std(act, n)
        act.wait_ge(ld_ctx1, 16)
        for k in range(KT):
            act.activation(ctx_h[:, k, HALF:2 * HALF], raw_b[:, k, :], ACT.Copy).then_inc(act_ctx, 1)
        for b in range(NB):
            act.wait_ge(h_ready, b + 1)
            if b >= 1:
                act.wait_ge(act_hsq, b)
            act.activation(score[:, 0, :], h_tok[:, b, :], ACT.Square, accum_out=ssq[:, 0, b:b + 1]).then_inc(act_hsq, 1)
        act.wait_ge(rms_step, 1)
        act.activation(ssq[:, 2, :], ssq[:, 1, :], ACT.Sqrt).then_inc(rms_std, 1)

        def split(m, g, k, free):
            if k == 0:
                act.wait_ge(ld[m], 16 * g + 16)
                if free is not None:
                    act.wait_ge(*free)
            scale = ln_w[:, k:k + 1] if m == "q" else 1.0
            act.activation(weights[m][0][:, k, :], raw[m][:, k, :], ACT.Copy, scale=scale).then_inc(act_w[m], 1)

        def evacuate(g, half, t):
            u = 2 * g + half
            act.wait_ge(pe_pr, PER * u + t + 1)
            act.activation(kqv[:, t, :], proj[t % RING][:, :], ACT.Copy).then_inc(act_pr, 1)

        def step(g, half, k, last=True):
            scored, _, _, _, out = parts(k)
            s0 = NB * g + BPH * half
            if out is not None:
                act.wait_ge(pe_y, s0 + out + 1)
                if any_later(g, half, out):
                    act.wait_ge(pe_o, s0 + out)
                act.activation(at[0][:, :], ps_y[:, :], ACT.Copy).then_inc(act_at, 1)
            if scored is not None:
                evacuate(g, half, TILES + scored)
                if half == 0 and scored < 3:
                    split("o", g, scored + 1, None)
                if half == 1 and not last:
                    split("q", g + 1, scored, (pe_pr, PER * (2 * g + 1) + TILES))
                s = s0 + scored
                act.wait_ge(dve_max, 2 * s + 2)
                if any_later(g, half, scored, 2):
                    act.wait_ge(dve_inv, 2 * s - 2)
                tile = score[:, scored % 3, :]
                for h in range(HPG):
                    cols = slice(h * P, (h + 1) * P)
                    act.activation(tile[:, cols], tile[:, cols], ACT.Exp, bias=neg_top[:, scored % 2, h:h + 1],
                                   accum_out=row_sum[:, scored % 2, h:h + 1]).then_inc(act_exp, 1)

        def unit(g, half, first, last):
            for t in range(TILES):
                if t % 2 == 0 and not first:
                    step(*before(g, half), BPH + t // 2)
                evacuate(g, half, t)
                if half == 0:
                    if t < KT:
                        split("v", g, t, None if first else (pe_pr, 2 * PER * g))
                    if t == TILES - 1:
                        split("o", g, 0, None if first else (pe_o, NB * g))
                elif t >= HPG and not last:
                    split("k", g + 1, t - HPG, (pe_pr, PER * (2 * g + 1) + HPG))
            for b in range(BPH):
                step(g, half, b, last)

        for m in "kq":
            for k in range(KT):
                split(m, 0, k, None)
        for b in range(NB):
            act.wait_ge(n.turned, b + 1)
            act.activation(act_h[:, :, b * P:(b + 1) * P], heads([ps_t, ps_o][b % 2][:, :]),
                           ACT.Copy).then_inc(n.high_ready, 1)
        unit(0, 0, True, False)
        unit(0, 1, False, False)
        with act.Fori(1, NG - 1) as g:
            unit(g, 0, False, False)
            unit(g, 1, False, False)
        unit(NG - 1, 0, False, True)
        unit(NG - 1, 1, False, True)
        for k in range(BPH, BPH + DRAIN):
            step(NG - 1, 1, k)

    @block.vector
    def _(dve):
        norm_vector_stats(dve, n, x_res)
        for b in range(NB):
            dve.tensor_scalar(h_tok[:, b, :], x_res[:, b, :], n.mv[:, b, 0:1], n.rs[:, b:b + 1],
                              ALU.subtract, ALU.mult).then_inc(h_ready, 1)
        for half, r in enumerate((raw_a, raw_b)):
            for k in range(KT):
                cols = slice(half * HALF, (half + 1) * HALF)
                dve.wait_ge(act_ctx, half * KT + k + 1)
                dve.tensor_tensor(ctx_l[:, k, cols], r[:, k, :], ctx_h[:, k, cols].bitcast(F32),
                                  ALU.subtract).then_inc(dve_ctx, 1)
        dve.wait_ge(h_ready, NB)
        for b in range(NB):
            dve.tensor_tensor(x_res[:, b, :], x_res[:, b, :], h_tok[:, b, :], ALU.add).then_inc(h_ready, 1)
        dve.wait_ge(act_hsq, NB)
        dve.tensor_scalar(ssq[:, 1, :], ssq[:, 0, :], 1.0 / HID, EPS, ALU.mult, ALU.add).then_inc(rms_step, 1)
        dve.wait_ge(rms_std, 1)
        dve.reciprocal(ssq[:, 3, :], ssq[:, 2, :]).then_inc(rms_step, 1)
        dve.wait_ge(rms_step, 2)
        dve.wait_ge(h_ready, 2 * NB)
        for b in range(NB):
            dve.tensor_scalar(h_tok[:, b, :], h_tok[:, b, :], ssq[:, 3, b:b + 1], None,
                              ALU.mult).then_inc(n.xn_ready, 1)
        dve.tensor_copy(ident_b[:, :], ident[:, :]).then_inc(const_ready, 1)
        dve.wait_ge(ld_mask, 16)
        dve.tensor_scalar(bar[:, :, :], mask_words[:, :, :].bitcast(U8), -1.0, -NEG, ALU.add, ALU.mult).then_inc(const_ready, 1)
        dve.wait_ge(ld_c, 16)

        def low(m, g, k):
            dve.wait_ge(act_w[m], KT * g + k + 1)
            if m == "q":
                dve.scalar_tensor_tensor(out=wq[1][:, k, :], in0=raw_b[:, k, :], scalar=ln_w[:, k:k + 1],
                                         in1=wq[0][:, k, :].bitcast(F32), op0=ALU.mult,
                                         op1=ALU.subtract).then_inc(dve_w[m], 1)
            else:
                dve.tensor_tensor(weights[m][1][:, k, :], raw[m][:, k, :], weights[m][0][:, k, :].bitcast(F32),
                                  ALU.subtract).then_inc(dve_w[m], 1)

        def step(g, half, k, last=True):
            scored, inverted, turned, _, out = parts(k)
            s0 = NB * g + BPH * half
            if out is not None:
                dve.wait_ge(act_at, s0 + out + 1)
                dve.tensor_tensor(at[1][:, :], ps_y[:, :], at[0][:, :].bitcast(F32), ALU.subtract).then_inc(dve_at, 1)
            if scored is not None:
                s = s0 + scored
                tile = score[:, scored % 3, :]
                dve.wait_ge(pe_s, s + 1)
                if half == 0 and scored == 0:
                    dve.wait_ge(ld_pos, 16 * g + 16)
                if scored == 3 or any_later(g, half, 0):
                    dve.wait_ge(pe_t, s0 + (1 if scored == 3 else 0))
                dve.tensor_tensor(tile, ps_s[:, :], pos[:, :, :].rearrange("p h k -> p (h k)"),
                                  ALU.add).then_inc(dve_sum, 1)
                dve.wait_ge(dve_sum, s + 1)
                dve.tensor_reduce(top[:, :], heads(tile), AX_X, ALU.max).then_inc(dve_max, 1)
                dve.wait_ge(dve_max, 2 * s + 1)
                if any_later(g, half, scored, 2):
                    dve.wait_ge(act_exp, HPG * (s - 1))
                dve.tensor_scalar(neg_top[:, scored % 2, :], top[:, :], 0.1 * NEG, -1.0, ALU.max,
                                  ALU.mult).then_inc(dve_max, 1)
                if half == 0 and scored < 3:
                    low("o", g, scored + 1)
                if half == 1 and not last:
                    low("q", g + 1, scored)
            if inverted is not None:
                s = s0 + inverted
                dve.wait_ge(act_exp, HPG * (s + 1))
                if any_later(g, half, inverted):
                    dve.wait_ge(dve_inv, 2 * s)
                dve.tensor_scalar(total[:, :], row_sum[:, inverted % 2, :], 1e-30, None,
                                  ALU.max).then_inc(dve_inv, 1)
                dve.wait_ge(dve_inv, 2 * s + 1)
                if any_later(g, half, inverted):
                    dve.wait_ge(pool_norm, s)
                dve.reciprocal(inverse[:, :], total[:, :]).then_inc(dve_inv, 1)
            if turned is not None:
                s = s0 + turned
                dve.wait_ge(pe_t, s + 1)
                if any_later(g, half, turned):
                    dve.wait_ge(pe_y, s)
                dve.tensor_copy(prob_t[:, :], ps_t[:, :]).then_inc(dve_pt, 1)
            if out is not None:
                dve.wait_ge(pe_o, s0 + out + 1)
                if any_later(g, half, out):
                    dve.wait_ge(dve_acc, s0 + out)
                b = BPH * half + out
                dve.tensor_tensor(x_res[:, b, :], x_res[:, b, :], ps_o[:, :], ALU.add).then_inc(dve_acc, 1)

        def unit(g, half, first, last):
            for t in range(TILES):
                if t % 2 == 0 and not first:
                    step(*before(g, half), BPH + t // 2)
                if half == 0:
                    if t < KT:
                        low("v", g, t)
                    if t == TILES - 1:
                        low("o", g, 0)
                elif t >= HPG and not last:
                    low("k", g + 1, t - HPG)
            for b in range(BPH):
                step(g, half, b, last)

        for m in "kq":
            for k in range(KT):
                low(m, 0, k)
        for b in range(NB):
            dve.wait_ge(n.high_ready, b + 1)
            cols = slice(b * P, (b + 1) * P)
            dve.tensor_tensor(act_l[:, :, cols], heads([ps_t, ps_o][b % 2][:, :]),
                              act_h[:, :, cols].bitcast(F32), ALU.subtract).then_inc(n.low_ready, 1)
        unit(0, 0, True, False)
        unit(0, 1, False, False)
        with dve.Fori(1, NG - 1) as g:
            unit(g, 0, False, False)
            unit(g, 1, False, False)
        unit(NG - 1, 0, False, True)
        unit(NG - 1, 1, False, True)
        for k in range(BPH, BPH + DRAIN):
            step(NG - 1, 1, k)

    @block.tensor
    def _(pe):
        norm_tensor_turn(pe, n, h_tok, ident, [ps_t, ps_o])
        pe.wait_ge(n.low_ready, NB)
        pe.wait_ge(n.high_ready, NB)
        pe.wait_ge(dve_ctx, 2 * KT)
        pe.wait_ge(const_ready, 2)

        def ring_free(g, half, t):
            u = 2 * g + half
            if half or t >= RING or not isinstance(g, int) or g > 0:
                pe.wait_ge(act_pr, PER * u + t - RING + 1)

        def tile(g, half, t):
            j = t % HPG
            m, rhs = ("k", (ctx_h, ctx_l)) if t < HPG else ("q", (act_h, act_l))
            wm = weights[m]
            if half == 0 and j == 0:
                pe.wait_ge(dve_w[m], KT * g + KT)
            ring_free(g, half, t)
            toks, cols = slice(half * HALF, (half + 1) * HALF), slice(j * P, (j + 1) * P)
            for k in range(KT):
                mm = product3(pe, proj[t % RING][:, :], (wm[0][:, k, cols], wm[1][:, k, cols]),
                              (rhs[0][:, k, toks], rhs[1][:, k, toks]), k == 0, k == KT - 1)
            mm.then_inc(pe_pr, 1)

        def v_tile(g, half, b):
            if half == 0 and b == 0:
                pe.wait_ge(dve_w["v"], KT * g + KT)
            ring_free(g, half, TILES + b)
            toks = slice((BPH * half + b) * P, (BPH * half + b + 1) * P)
            for k in range(KT):
                mm = product3(pe, proj[(TILES + b) % RING][:, :], (ctx_h[:, k, toks], ctx_l[:, k, toks]),
                              (wv[0][:, k, :], wv[1][:, k, :]), k == 0, k == KT - 1)
            mm.then_inc(pe_pr, 1)

        def step(g, half, k):
            scored, _, turned, mixed, out = parts(k)
            u, s0 = 2 * g + half, NB * g + BPH * half
            if scored is not None:
                s = s0 + scored
                v_tile(g, half, scored)
                if scored == 0:
                    pe.wait_ge(act_pr, PER * u + TILES)
                if any_later(g, half, scored):
                    pe.wait_ge(dve_sum, s)
                pe.matmul(ps_s[:, :], ident_b[:, :], bar[:, BPH * half + scored, :].unsqueeze(1).broadcast_to([P, HPG, P]),
                          start=True, stop=False, skip_group_check=True)
                toks = slice(scored * P, (scored + 1) * P)
                for h in range(HPG):
                    mm = pe.matmul(ps_s[:, h * P:(h + 1) * P], q_t[:, h, toks], k_t[:, h, toks],
                                   start=False, stop=h == HPG - 1, skip_group_check=True)
                mm.then_inc(pe_s, 1)
            if turned is not None:
                s = s0 + turned
                pe.wait_ge(pool_norm, s + 1)
                if any_later(g, half, turned):
                    pe.wait_ge(dve_pt, s)
                for h in range(HPG):
                    cols = slice(h * P, (h + 1) * P)
                    mm = pe.transpose(ps_t[:, cols], score[:, turned % 3, cols], ident[:, :])
                mm.then_inc(pe_t, 1)
            if out is not None:
                s = s0 + out
                if half == 0 and out == 0:
                    pe.wait_ge(dve_w["o"], KT * g + KT)
                pe.wait_ge(dve_at, s + 1)
                if any_later(g, half, out):
                    pe.wait_ge(dve_acc, s)
                for h in range(HPG):
                    cols = slice(h * P, (h + 1) * P)
                    mm = product3(pe, ps_o[:, :], (at[0][:, cols], at[1][:, cols]), (wo[0][:, h, :], wo[1][:, h, :]),
                                  h == 0, h == HPG - 1)
                mm.then_inc(pe_o, 1)
            if mixed is not None:
                s = s0 + mixed
                pe.wait_ge(dve_pt, s + 1)
                pe.wait_ge(act_pr, PER * u + TILES + mixed + 1)
                if any_later(g, half, mixed):
                    pe.wait_ge(dve_at, s)
                for h in range(HPG):
                    cols = slice(h * P, (h + 1) * P)
                    mm = pe.matmul(ps_y[:, cols], v_tok[:, mixed, cols], prob_t[:, cols], start=True, stop=True)
                mm.then_inc(pe_y, 1)

        def unit(g, half, first):
            for t in range(TILES):
                tile(g, half, t)
                if t % 2 == 0 and not first:
                    step(*before(g, half), BPH + t // 2)
            for b in range(BPH):
                step(g, half, b)

        unit(0, 0, True)
        unit(0, 1, False)
        with pe.Fori(1, NG) as g:
            unit(g, 0, False)
            unit(g, 1, False)
        for k in range(BPH, BPH + DRAIN):
            step(NG - 1, 1, k)


def experts(nc, ctx, x_res, act_h, act_l, ident, const, w, out_dram):

    def sb(name, shape, dt):
        return ctx.enter_context(nc.sbuf_tensor(f"m_{name}", shape, dt))

    def sem(name):
        return ctx.enter_context(nc.semaphore(f"m_{name}"))

    def psum(name):
        return ctx.enter_context(nc.psum_tensor(f"m_ps_{name}", [P, 512], F32))

    PAIRS = NCOMB // 2
    raw_gu = sb("raw_gu", [P, 2, KT, HALF], F32)
    raw_d = sb("raw_d", [P, 2, 2, HID], F32)
    wgu = [sb(f"wgu_{s}", [P, 2, KT, HALF], F32R) for s in ("high", "low")]
    wd = [sb(f"wd_{s}", [P, 2, 2, HID], F32R) for s in ("high", "low")]
    zt = [sb(f"z_{s}", [P, 2, 2, NB * P], F32R) for s in ("high", "low")]
    silu = sb("silu", [P, 2, HALF], F32)
    z = sb("z", [P, 2, HALF], F32)
    xn = sb("xn", [P, NB, HID], F32)
    router_raw = sb("router_raw", [P, KT, NEXP], F32)
    router = [sb(f"router_{s}", [P, KT, NEXP], F32R) for s in ("high", "low")]
    pick_raw = sb("pick_raw", [3 * NH, NH], F32)
    pick = sb("pick", [3 * NH, NH], BF16)
    order = sb("order", [P, NEXP], F32)
    logit, prob, rest, hit, first_hit, second_hit, weigh = (
        sb(s, [P, NB, NEXP], F32) for s in ("logit", "prob", "rest", "hit", "first_hit", "second_hit", "weigh"))
    col = sb("col", [P, 8, NB], F32)
    comb = sb("comb", [P, NB, NCOMB], F32)
    comb3 = sb("comb3", [3 * NH, NB * P], BF16)
    piece = xn[0:NCOMB, 0, :].bitcast(BF16)
    left = xn[0:NCOMB, 1:3, :].rearrange("p a n -> p (a n)")

    ps_g, ps_u = [psum("g0"), psum("g1")], [psum("u0"), psum("u1")]
    ps_c = psum("weight")
    ps_o = [psum("out0"), psum("out1")]

    n = Norm(sb, sem, "ffn")
    ld_c, ld_gu, ld_d = sem("ld_c"), [sem("ld_gu0"), sem("ld_gu1")], [sem("ld_d0"), sem("ld_d1")]
    const_ready, act_router, dve_router = sem("const_ready"), sem("act_router"), sem("dve_router")
    pe_logit, route, act_route, pe_comb, comb_ready = (sem("pe_logit"), sem("route"), sem("act_route"),
                                                       sem("pe_comb"), sem("comb_ready"))
    act_gu, dve_gu, act_d, dve_d = sem("act_gu"), sem("dve_gu"), sem("act_d"), sem("dve_d")
    pe_g, pe_u, pe_c, pe_o = sem("pe_g"), sem("pe_u"), sem("pe_c"), sem("pe_o")
    act_silu, dve_weighed, dve_z, act_zh, pool_zl, dve_acc = (sem("act_silu"), sem("dve_weighed"), sem("dve_z"),
                                                              sem("act_zh"), sem("pool_zl"), sem("dve_acc"))
    zero_ready, stored = sem("zero_ready"), sem("stored")
    STEPS = 4

    def loops(eng, body):
        body(0, 0, True, False)
        body(1, 1, False, False)
        with eng.Fori(1, PAIRS // 2 - 1) as turn:
            body(2 * turn, 0, False, False)
            body(2 * turn + 1, 1, False, False)
        body(PAIRS - 2, 0, False, False)
        body(PAIRS - 1, 1, False, True)

    def at_start(p, j, lag=1):
        return isinstance(p, int) and STEPS * p + j < lag

    block = ctx.enter_context(nc.Block())

    @block.sync
    def _(sp):
        sp.dma_start(router_raw[:, :, :], w["router"]).then_inc(ld_c, 16)
        sp.dma_start(pick_raw[:, :], const["pick"]).then_inc(ld_c, 16)
        sp.dma_start(order[:, :], const["order"]).then_inc(ld_c, 16)

        def load(p, parity, wait):
            if wait:
                sp.wait_ge(dve_gu, KT * (p - 1))
            sp.dma_start(raw_gu[:, parity, :, :], w["gu"][bass.ds(p, 1)].rearrange("e p k n -> p (e k) n")).then_inc(ld_gu[parity], 16)
            if wait:
                sp.wait_ge(dve_d, 2 * (p - 1))
            sp.dma_start(raw_d[:, parity, :, :], w["down"][bass.ds(p, 1)].rearrange("e p k n -> p (e k) n")).then_inc(ld_d[parity], 16)

        load(0, 0, False)
        load(1, 1, False)
        with sp.Fori(1, PAIRS // 2) as turn:
            load(2 * turn, 0, True)
            load(2 * turn + 1, 1, True)
        for b in range(NB):
            sp.wait_ge(dve_acc, NB * (PAIRS - 1) + b + 1)
            sp.dma_start(out_dram[b], x_res[:, b, :]).then_inc(stored, 16)
        sp.wait_ge(stored, 16 * NB)

    @block.gpsimd
    def _(pool):
        pool.memset(comb3[:, :], 0.0).then_inc(zero_ready, 1)
        pool.memset(comb[:, :, NEXP:NCOMB], 1.0).then_inc(zero_ready, 1)

        def body(p, parity, first, last):
            for j in range(STEPS):
                s = STEPS * p + j
                toks = slice((j % 2) * HALF, (j % 2 + 1) * HALF)
                pool.wait_ge(act_zh, s + 1)
                pool.tensor_tensor(zt[1][:, parity, j // 2, toks], z[:, j % 2, :],
                                   zt[0][:, parity, j // 2, toks].bitcast(F32), ALU.subtract).then_inc(pool_zl, 1)

        loops(pool, body)

    @block.scalar
    def _(act):
        norm_scalar_std(act, n)
        act.wait_ge(ld_c, 48)
        act.activation(router[0][:, :, :], router_raw[:, :, :], ACT.Copy).then_inc(act_router, 1)

        def split_gu(p, parity, k):
            if k == 0:
                act.wait_ge(ld_gu[parity], load_count(p, parity))
                if not (isinstance(p, int) and p < 2):
                    act.wait_ge(pe_u, STEPS * (p - 1))
            act.activation(wgu[0][:, parity, k, :], raw_gu[:, parity, k, :], ACT.Copy).then_inc(act_gu, 1)

        def split_d(p, parity, k):
            if k == 0:
                act.wait_ge(ld_d[parity], load_count(p, parity))
                if not (isinstance(p, int) and p < 2):
                    act.wait_ge(pe_o, NB * (p - 1))
            act.activation(wd[0][:, parity, k, :], raw_d[:, parity, k, :], ACT.Copy).then_inc(act_d, 1)

        def load_count(p, parity):
            return 8 * p + 16 if parity == 0 else 8 * p + 8

        for k in range(KT):
            split_gu(0, 0, k)
        for b in range(NB):
            act.wait_ge(n.turned, b + 1)
            act.activation(act_h[:, :, b * P:(b + 1) * P], heads(ps_o[b % 2][:, :]),
                           ACT.Copy).then_inc(n.high_ready, 1)
        act.wait_ge(route, 3)
        act.activation(prob[:, :, :], rest[:, :, :], ACT.Exp).then_inc(act_route, 1)

        def high_z(p, parity, j):
            s = STEPS * p + j
            toks = slice((j % 2) * HALF, (j % 2 + 1) * HALF)
            act.wait_ge(dve_z, s + 1)
            if j == 0 and not (isinstance(p, int) and p < 2):
                act.wait_ge(pe_o, NB * (p - 1))
            act.activation(zt[0][:, parity, j // 2, toks], z[:, j % 2, :], ACT.Copy).then_inc(act_zh, 1)

        def body(p, parity, first, last):
            for j in range(STEPS):
                s = STEPS * p + j
                if j > 0:
                    high_z(p, parity, j - 1)
                elif not first:
                    high_z(p - 1, 1 - parity, STEPS - 1)
                act.wait_ge(pe_g, s + 1)
                if not at_start(p, j, 2):
                    act.wait_ge(dve_z, s - 1)
                act.activation(silu[:, j % 2, :], ps_g[j % 2][:, :], ACT.Silu).then_inc(act_silu, 1)
                if not last:
                    split_gu(p + 1, 1 - parity, j)
                if j >= 2:
                    split_d(p, parity, j - 2)

        loops(act, body)
        high_z(PAIRS - 1, 1, STEPS - 1)

    @block.vector
    def _(dve):
        norm_vector_stats(dve, n, x_res)
        for b in range(NB):
            dve.tensor_scalar(xn[:, b, :], x_res[:, b, :], n.mv[:, b, 0:1], n.rs[:, b:b + 1],
                              ALU.subtract, ALU.mult).then_inc(n.xn_ready, 1)
        dve.wait_ge(ld_c, 48)
        dve.tensor_copy(pick[:, :], pick_raw[:, :]).then_inc(const_ready, 1)
        dve.wait_ge(act_router, 1)
        dve.tensor_tensor(router[1][:, :, :], router_raw[:, :, :], router[0][:, :, :].bitcast(F32),
                          ALU.subtract).then_inc(dve_router, 1)

        def low_gu(p, parity, k):
            dve.wait_ge(act_gu, KT * p + k + 1)
            dve.tensor_tensor(wgu[1][:, parity, k, :], raw_gu[:, parity, k, :], wgu[0][:, parity, k, :].bitcast(F32),
                              ALU.subtract).then_inc(dve_gu, 1)

        def low_d(p, parity, k):
            dve.wait_ge(act_d, 2 * p + k + 1)
            dve.tensor_tensor(wd[1][:, parity, k, :], raw_d[:, parity, k, :], wd[0][:, parity, k, :].bitcast(F32),
                              ALU.subtract).then_inc(dve_d, 1)

        for k in range(KT):
            low_gu(0, 0, k)
        for b in range(NB):
            dve.wait_ge(n.high_ready, b + 1)
            cols = slice(b * P, (b + 1) * P)
            dve.tensor_tensor(act_l[:, :, cols], heads(ps_o[b % 2][:, :]),
                              act_h[:, :, cols].bitcast(F32), ALU.subtract).then_inc(n.low_ready, 1)

        def spread(c):
            return c.unsqueeze(2).broadcast_to([P, NB, NEXP])

        count = [0]

        def done(instruction):
            instruction.then_inc(route, 1)
            count[0] += 1

        top, total, inverse, v1, key1, v2, key2, both = (col[:, i, :] for i in range(8))
        ordered = order[:, :].unsqueeze(1).broadcast_to([P, NB, NEXP])
        dve.wait_ge(pe_logit, 1)
        done(dve.tensor_copy(logit[:, :, :], ps_c[:, 0:NB * NEXP].rearrange("p (b e) -> p b e", b=NB)))
        dve.wait_ge(route, 1)
        done(dve.tensor_reduce(top, logit[:, :, :], AX_X, ALU.max))
        dve.wait_ge(route, 2)
        done(dve.tensor_tensor(rest[:, :, :], logit[:, :, :], spread(top), ALU.subtract))
        dve.wait_ge(act_route, 1)
        done(dve.tensor_reduce(total, prob[:, :, :], AX_X, ALU.add))
        dve.wait_ge(route, 4)
        done(dve.reciprocal(inverse, total))
        dve.wait_ge(route, 5)
        done(dve.tensor_tensor(prob[:, :, :], prob[:, :, :], spread(inverse), ALU.mult))
        left_over = prob
        for best, key, one in ((v1, key1, first_hit), (v2, key2, second_hit)):
            dve.wait_ge(route, count[0])
            done(dve.tensor_reduce(best, left_over[:, :, :], AX_X, ALU.max))
            dve.wait_ge(route, count[0])
            done(dve.tensor_tensor(hit[:, :, :], left_over[:, :, :], spread(best), ALU.is_equal))
            dve.wait_ge(route, count[0])
            done(dve.tensor_tensor(hit[:, :, :], hit[:, :, :], ordered, ALU.mult))
            dve.wait_ge(route, count[0])
            done(dve.tensor_reduce(key, hit[:, :, :], AX_X, ALU.max))
            dve.wait_ge(route, count[0])
            done(dve.tensor_tensor(one[:, :, :], hit[:, :, :], spread(key), ALU.is_equal))
            if best is v1:
                dve.wait_ge(route, count[0])
                done(dve.scalar_tensor_tensor(out=rest[:, :, :], in0=one[:, :, :], scalar=-2.0, in1=prob[:, :, :],
                                              op0=ALU.mult, op1=ALU.add))
                left_over = rest
        dve.wait_ge(route, count[0])
        done(dve.tensor_tensor(weigh[:, :, :], first_hit[:, :, :], second_hit[:, :, :], ALU.add))
        done(dve.tensor_tensor(both, v1, v2, ALU.add))
        dve.wait_ge(route, count[0])
        done(dve.tensor_tensor(weigh[:, :, :], weigh[:, :, :], prob[:, :, :], ALU.mult))
        done(dve.reciprocal(both, both))
        dve.wait_ge(route, count[0])
        dve.wait_ge(zero_ready, 2)
        done(dve.tensor_tensor(comb[:, :, 0:NEXP], weigh[:, :, :], spread(both), ALU.mult))
        assert count[0] == ROUTE_STEPS
        dve.wait_ge(pe_comb, 1)
        for half in range(2):
            done(dve.tensor_copy(left[:, half * HALF:(half + 1) * HALF], ps_o[half][0:NCOMB, :]))
        for i in range(3):
            dve.wait_ge(route, count[0])
            done(dve.tensor_copy(piece, left))
            dve.wait_ge(route, count[0])
            done(dve.tensor_copy(comb3[i * NH:i * NH + NCOMB, :], piece))
            if i < 2:
                done(dve.tensor_tensor(left, left, piece, ALU.subtract))
        dve.wait_ge(route, count[0])
        assert count[0] == COMB_STEPS

        def body(p, parity, first, last):
            for j in range(STEPS):
                s = STEPS * p + j
                tile = silu[:, j % 2, :]
                dve.wait_ge(act_silu, s + 1)
                dve.wait_ge(pe_c, s + 1)
                dve.tensor_tensor(tile, tile, ps_c[:, :], ALU.mult).then_inc(dve_weighed, 1)
                dve.wait_ge(dve_weighed, s + 1)
                dve.wait_ge(pe_u, s + 1)
                if not at_start(p, j, 2):
                    dve.wait_ge(pool_zl, s - 1)
                dve.tensor_tensor(z[:, j % 2, :], tile, ps_u[j % 2][:, :], ALU.mult).then_inc(dve_z, 1)
                if not last:
                    low_gu(p + 1, 1 - parity, j)
                if not first:
                    accumulate(p - 1, 2 * j)
                    accumulate(p - 1, 2 * j + 1)
                if j >= 2:
                    low_d(p, parity, j - 2)

        def accumulate(p, b):
            m = NB * p + b
            dve.wait_ge(pe_o, m + 1)
            if not (isinstance(p, int) and m == 0):
                dve.wait_ge(dve_acc, m)
            dve.tensor_tensor(x_res[:, b, :], x_res[:, b, :], ps_o[b % 2][:, :], ALU.add).then_inc(dve_acc, 1)

        loops(dve, body)
        for b in range(NB):
            accumulate(PAIRS - 1, b)

    @block.tensor
    def _(pe):
        norm_tensor_turn(pe, n, xn, ident, ps_o)
        pe.wait_ge(n.low_ready, NB)
        pe.wait_ge(n.high_ready, NB)
        pe.wait_ge(dve_router, 1)
        for b in range(NB):
            toks = slice(b * P, (b + 1) * P)
            for k in range(KT):
                mm = product3(pe, ps_c[:, b * NEXP:(b + 1) * NEXP], (act_h[:, k, toks], act_l[:, k, toks]),
                              (router[0][:, k, :], router[1][:, k, :]), k == 0, k == KT - 1)
        mm.then_inc(pe_logit, 1)

        def gate_up(p, parity, j, which):
            s = STEPS * p + j
            bank, used, made = ((ps_g, act_silu, pe_g), (ps_u, dve_z, pe_u))[which]
            if j == 0 and which == 0:
                pe.wait_ge(dve_gu, KT * p + KT)
            if not at_start(p, j, 2):
                pe.wait_ge(used, s - 1)
            toks = slice((j % 2) * HALF, (j % 2 + 1) * HALF)
            cols = slice((2 * (j // 2) + which) * P, (2 * (j // 2) + which + 1) * P)
            for k in range(KT):
                mm = product3(pe, bank[j % 2][:, :], (wgu[0][:, parity, k, cols], wgu[1][:, parity, k, cols]),
                              (act_h[:, k, toks], act_l[:, k, toks]), k == 0, k == KT - 1)
            mm.then_inc(made, 1)

        def combine(p, j):
            s = STEPS * p + j
            if not at_start(p, j):
                pe.wait_ge(dve_weighed, s)
            pe.matmul(ps_c[:, :], pick[:, bass.ds(2 * p + j // 2, 1)].broadcast_to([3 * NH, P]),
                      comb3[:, (j % 2) * HALF:(j % 2 + 1) * HALF], start=True, stop=True).then_inc(pe_c, 1)

        def down(p, parity, b):
            m = NB * p + b
            if b == 0:
                pe.wait_ge(dve_d, 2 * p + 2)
                pe.wait_ge(pool_zl, STEPS * p + STEPS)
            if not (isinstance(p, int) and m < 2):
                pe.wait_ge(dve_acc, m - 1)
            toks = slice(b * P, (b + 1) * P)
            for e in range(2):
                mm = product3(pe, ps_o[b % 2][:, :], (zt[0][:, parity, e, toks], zt[1][:, parity, e, toks]),
                              (wd[0][:, parity, e, :], wd[1][:, parity, e, :]), e == 0, e == 1)
            mm.then_inc(pe_o, 1)

        def body(p, parity, first, last):
            for j in range(STEPS):
                gate_up(p, parity, j, 0)
                gate_up(p, parity, j, 1)
                if first and j == 0:
                    turn_weights()
                combine(p, j)
                if not first:
                    down(p - 1, 1 - parity, 2 * j)
                    down(p - 1, 1 - parity, 2 * j + 1)

        def turn_weights():
            pe.wait_ge(route, ROUTE_STEPS)
            for b in range(NB):
                mm = pe.transpose(ps_o[b // BPH][0:NCOMB, (b % BPH) * P:(b % BPH + 1) * P], comb[:, b, :], ident[:, :])
            mm.then_inc(pe_comb, 1)
            pe.wait_ge(route, COMB_STEPS)
            pe.wait_ge(const_ready, 1)

        loops(pe, body)
        for b in range(NB):
            down(PAIRS - 1, 1, b)


def decoder_layer(nc, x, context, mask, out, const, w):
    with ExitStack() as ctx:
        x_res = ctx.enter_context(nc.sbuf_tensor("x_res", [P, NB, HID], F32))
        act_h = ctx.enter_context(nc.sbuf_tensor("act_high", [P, KT, NB * P], F32R))
        act_l = ctx.enter_context(nc.sbuf_tensor("act_low", [P, KT, NB * P], F32R))
        ident = ctx.enter_context(nc.sbuf_tensor("ident", [P, P], F32))
        with ExitStack() as phase:
            self_attention(nc, phase, x_res, act_h, act_l, ident, const, w, x)
        with ExitStack() as phase:
            cross_attention(nc, phase, x_res, act_h, act_l, ident, const, w, context, mask)
        with ExitStack() as phase:
            experts(nc, phase, x_res, act_h, act_l, ident, const, w, out)


def _lay_out(inputs):
    import numpy as np

    a = {k: np.asarray(v) for k, v in inputs.items()}

    def by_rows(w, groups):
        return w.reshape(groups, -1, KT, P).transpose(0, 3, 2, 1)

    def by_cols(w):
        return w.reshape(HID, NG, HPG, P).transpose(1, 3, 2, 0)

    w = {
        "Wqk": np.concatenate([by_rows(a["L0_attn_Wk"], NG), by_rows(a["L0_attn_Wq"], NG)], axis=3),
        "Wv": by_rows(a["L0_attn_Wv"], 2),
        "Wg": by_rows(a["L0_attn_Wg"], NG),
        "Wo": by_cols(a["L0_attn_Wo"]),
        "Win": by_rows(a["L0_attn_Win"], 1)[0],
        "gnorm": a["L0_attn_gnorm_w"].reshape(P, 1),
        "dt_bias": a["L0_attn_dt_bias"].reshape(NH, 1),
        "A_log": a["L0_attn_A_log_bias"].reshape(NH, 1),
    }
    for m in "qkv":
        w[f"X{m}"] = by_rows(a[f"L0_xattn_w_{m}"], NG)
    w["Xo"] = by_cols(a["L0_xattn_w_out"])
    w["ln_w"] = a["L0_xattn_ln_weight"].reshape(KT, P).T
    w["pos"] = a["L0_xattn_position_bias"].reshape(NG, HPG, P, P).transpose(0, 2, 1, 3)
    gate_up = a["L0_ffn_w_gate_up"].reshape(NEXP, 2, P, HID)
    shared = a["L0_ffn_shared_w_gate_up"].reshape(2, HPG, P, HID).transpose(1, 0, 2, 3)
    w["gu"] = by_rows(np.concatenate([gate_up, shared]), NCOMB // 2)
    down = a["L0_ffn_w_down"].transpose(0, 2, 1)
    shared = a["L0_ffn_shared_w_down"].T.reshape(HPG, P, HID)
    w["down"] = np.concatenate([down, shared]).reshape(NCOMB // 2, 2, P, HID).transpose(0, 2, 1, 3)
    w["router"] = by_rows(a["L0_ffn_gate_w"], 1)[0]
    a["context"] = by_rows(a["ctx_4096"], 2)
    a["mask"] = np.ascontiguousarray(a["mask_BxSxS2_bk0"].transpose(1, 0, 2)).view(np.int32)
    freq = np.float32(1.0) / np.float32(10000.0) ** (np.arange(0, P, 2, dtype=np.float32) / np.float32(P))
    angle = (np.arange(P, dtype=np.float32)[:, None] * freq).T
    key, query = np.arange(P)[:, None], np.arange(P)[None, :]
    const = {
        "ident": np.eye(P, dtype=np.float32),
        "cos": np.concatenate([np.cos(angle), np.cos(angle)]),
        "sin": np.concatenate([-np.sin(angle), np.sin(angle)]),
        "causal": np.tile(np.where(query >= key, 0.0, NEG).astype(np.float32), (1, HPG)),
        "order": np.tile(np.arange(NEXP, 0, -1, dtype=np.float32), (P, 1)),
        "pick": np.tile(np.eye(NH, dtype=np.float32), (3, 1)),
    }
    return a, w, const


def kernel(**inputs):
    import numpy as _np
    import concourse.bacc as _bacc
    from concourse import mybir as _mybir
    from concourse.bass_utils import run_bass_kernel_spmd as _run

    a, w, const = _lay_out(inputs)
    nc = _bacc.Bacc("TRN2", target_bir_lowering=False, num_devices=1)
    arrays = {}

    def dram(name, array):
        arrays[name] = _np.ascontiguousarray(array)
        return nc.dram_tensor(name, arrays[name].shape, _mybir.dt.from_np(arrays[name].dtype), kind="ExternalInput").ap()

    x = dram("in_x", a["x"])
    context, mask = dram("in_context", a["context"]), dram("in_mask", a["mask"])
    w = {k: dram(f"in_{k}", v) for k, v in w.items()}
    const = {k: dram(f"const_{k}", v) for k, v in const.items()}
    out = nc.dram_tensor("out_0", a["x"].shape, _mybir.dt.float32, kind="ExternalOutput").ap()
    decoder_layer(nc, x, context, mask, out, const, w)
    r = _run(nc, [arrays], core_ids=[0])
    return r.results[0]["out_0"]
```

```python
from contextlib import ExitStack

import concourse.bass as bass
from concourse import mybir

F32 = mybir.dt.float32
F32R = mybir.dt.float32r
BF16 = mybir.dt.bfloat16
I32 = mybir.dt.int32
U8 = mybir.dt.uint8
ALU = mybir.AluOpType
ACT = mybir.ActivationFunctionType
AX_X = mybir.AxisListType.X

P = 128
NB = 8
HID = 512
KT = HID // P
HALF = 512
BPH = HALF // P
HPG = 4
NG = 8
NH = NG * HPG
NEXP = 16
NCOMB = NEXP + HPG
NU = NCOMB // HPG
EPS = 1e-5
NEG = -1e30
TILES_QK = 2 * (1 + HPG)
FIRST_TILES = 1 + HPG
STEP_TILES = {0: (5, 6), 1: (7,), 2: (8,), 3: (9,)}
STEP_SPLITS = {4: (0, 1), 5: (2,), 6: (3,)}
RING = 3
NEWTON = 3
RSQRT_MAGIC = 0x5F3759DF
ROUTE_STEPS = 27
DT_STEPS = 18 + NB


def later(g, b, lag=1):
    return not isinstance(g, int) or NB * g + b >= lag


def before(g, half):
    return (g, 0) if half else (g - 1, 1)


def per_head(column, width=P):
    return column.unsqueeze(2).broadcast_to([column.shape[0], column.shape[1], width])


def heads(tile):
    return tile.rearrange("p (h d) -> p h d", h=HPG)


def product3(pe, out, left, right, first, last):
    (lh, ll), (rh, rl) = left, right
    pe.matmul(out, lh, rh, start=first, stop=False)
    pe.matmul(out, lh, rl, start=False, stop=False)
    return pe.matmul(out, ll, rh, start=False, stop=last)


class Norm:

    def __init__(self, sb, sem, tag):
        self.st = sb(f"{tag}_stats", [P, NB, 6], F32)
        self.mv = sb(f"{tag}_mean_var", [P, NB, 2], F32)
        self.ve = sb(f"{tag}_var_eps", [P, NB], F32)
        self.sd = sb(f"{tag}_std", [P, NB], F32)
        self.rs = sb(f"{tag}_rstd", [P, NB], F32)
        self.stats_done = sem(f"{tag}_stats_done")
        self.var_ready = sem(f"{tag}_var_ready")
        self.std_ready = sem(f"{tag}_std_ready")
        self.rstd_ready = sem(f"{tag}_rstd_ready")
        self.xn_ready = sem(f"{tag}_xn_ready")
        self.turned = sem(f"{tag}_turned")
        self.high_ready = sem(f"{tag}_high_ready")
        self.low_ready = sem(f"{tag}_low_ready")


def norm_block_stats(dve, n, x_res, b):
    dve.bn_stats(n.st[:, b, :], x_res[:, b, :]).then_inc(n.stats_done, 1)


def norm_vector_rstd(dve, n):
    dve.wait_ge(n.stats_done, NB)
    for b in range(NB):
        dve.bn_aggr(n.mv[:, b, :], n.st[:, b, :]).then_inc(n.stats_done, 1)
    dve.wait_ge(n.stats_done, 2 * NB)
    dve.tensor_scalar(n.ve[:, :], n.mv[:, :, 1], EPS, None, ALU.add).then_inc(n.var_ready, 1)
    dve.wait_ge(n.std_ready, 1)
    dve.reciprocal(n.rs[:, :], n.sd[:, :]).then_inc(n.rstd_ready, 1)
    dve.wait_ge(n.rstd_ready, 1)


def norm_scalar_std(act, n, count=1):
    act.wait_ge(n.var_ready, count)
    act.activation(n.sd[:, :], n.ve[:, :], ACT.Sqrt).then_inc(n.std_ready, 1)


def norm_tensor_turn(pe, n, xn, ident, banks, blocks=range(NB)):
    for b in blocks:
        pe.wait_ge(n.xn_ready, b + 1)
        if b >= len(banks):
            pe.wait_ge(n.low_ready, b - len(banks) + 1)
        for k in range(KT):
            mm = pe.transpose(banks[b % len(banks)][:, k * P:(k + 1) * P], xn[:, b, k * P:(k + 1) * P], ident[:, :])
        mm.then_inc(n.turned, 1)


def self_attention(nc, ctx, x_res, act_h, act_l, ident, norms, raw_a, raw_b, ld_ctx0, ld_wk, const, w, x_dram, context):

    def sb(name, shape, dt):
        return ctx.enter_context(nc.sbuf_tensor(name, shape, dt))

    def sem(name):
        return ctx.enter_context(nc.semaphore(name))

    def psum(name):
        return ctx.enter_context(nc.psum_tensor(name, [P, 512], F32))

    QK = (HPG + 1) * P
    wqk = [sb(f"wqk_{s}", [P, KT, QK], F32R) for s in ("high", "low")]
    wg = [sb(f"wg_{s}", [P, KT, HALF], F32R) for s in ("high", "low")]
    wo = [sb(f"wo_{s}", [P, HPG, HID], F32R) for s in ("high", "low")]
    gnorm = sb("gnorm", [P, 2], F32)
    cos = sb("cos", [P, P], F32)
    sin = sb("sin", [P, P], F32)
    causal = sb("causal", [P, HPG * P], BF16)
    ident_b = sb("ident_b", [P, P], BF16)
    pick = sb("pick", [3 * NH, NH], BF16)
    cum3 = sb("cum3", [3 * NH, NB * P], BF16)
    bias = sb("bias", [P, NB, NH], F32)
    v_tok = sb("v_tok", [P, NB, NG * P], F32)
    q_t = sb("q_t", [P, 2, HPG, HALF], F32)
    k_t = sb("k_t", [P, 2, HALF], F32)
    turned_q = sb("turned_q", [P, 2, HALF], F32)
    tanh = sb("tanh", [P, HALF], F32)
    gate = sb("gate", [P, 2, HALF], F32)
    decay = sb("decay", [P, HALF], F32)
    prob = sb("prob", [P, 2, HALF], F32)
    square = sb("square", [P, HALF], F32)
    z = sb("z", [P, 2, HALF], F32)
    zt = [sb(f"zt_{s}", [P, HALF], F32R) for s in ("high", "low")]
    ssq = sb("ssq", [P, 8, HPG], F32)

    proj = [psum(f"ps_proj{i}") for i in range(RING)]
    ps_d, ps_s, ps_y, ps_t, ps_o = (psum(f"ps_{n}") for n in ("decay", "scores", "y", "turn", "out"))

    n, next_norm = norms
    norm_banks = [ps_t, ps_o, ps_s, ps_y]
    ld_x = [sem(f"ld_x{i}") for i in range(NB // 2)]
    ld_c, ld_dt = sem("ld_c"), sem("ld_dt")
    ld_v0, ld_v1, ld_qk, ld_g, ld_o = sem("ld_v0"), sem("ld_v1"), sem("ld_qk"), sem("ld_g"), sem("ld_o")
    zero_ready, const_ready = sem("zero_ready"), sem("const_ready")
    act_wv, dve_wv = sem("act_wv"), sem("dve_wv")
    act_win, dve_win = sem("act_win"), sem("dve_win")
    act_wqk, dve_wqk = sem("act_wqk"), sem("dve_wqk")
    act_wg, dve_wg = sem("act_wg"), sem("dve_wg")
    act_wo, dve_wo = sem("act_wo"), sem("dve_wo")
    pe_dt, dt_step, act_dt = sem("pe_dt"), sem("dt_step"), sem("act_dt")
    pe_bias, bias_ready = sem("pe_bias"), sem("bias_ready")
    pe_v, act_v = sem("pe_v"), sem("act_v")
    pe_qk, pe_g, pe_d, pe_s, pe_y, pe_t, pe_o = (sem(f"pe_{s}") for s in ("qk", "g", "d", "s", "y", "t", "o"))
    dve_cos, act_turn, pool_sin, dve_rope = sem("dve_cos"), sem("act_turn"), sem("pool_sin"), sem("dve_rope")
    act_tanh, dve_gate, act_decay, dve_prob = sem("act_tanh"), sem("dve_gate"), sem("act_decay"), sem("dve_prob")
    act_square, dve_ssq, pool_newton, pool_z = sem("act_square"), sem("dve_ssq"), sem("pool_newton"), sem("pool_z")
    dve_z, act_zt, dve_zt, dve_acc = sem("dve_z"), sem("act_zt"), sem("dve_zt"), sem("dve_acc")

    win_raw = raw_b[:, :, 0:NH]
    win = [wqk[s][:, :, 0:P] for s in (0, 1)]

    def rows(i):
        return q_t[0:NH, i // 2, 2 * (i % 2):2 * (i % 2) + 2, :].rearrange("p a n -> p (a n)")

    z_row, e_row, dt_row, cum_row = rows(0), rows(1), rows(2), rows(3)
    k_rows = k_t[0:NH, :, :].rearrange("p a n -> p (a n)")
    t_rows = turned_q[0:NH, :, :].rearrange("p a n -> p (a n)")
    piece = prob[0:NH, 0, :].bitcast(BF16)
    head_col = sb("head_col", [NH, 4], F32)
    xn = v_tok[:, :, 0:HID]

    order = [("qk", t) for t in range(FIRST_TILES)]
    for step in range(NB):
        order += [("gate", step)] + [("qk", t) for t in STEP_TILES.get(step, ())]

    def ring_bank(kind, i):
        return proj[order.index((kind, i)) % RING]

    block = ctx.enter_context(nc.Block())

    @block.sync
    def _(sp):
        for b in range(0, NB, 2):
            sp.dma_start(x_res[:, b:b + 2, :], x_dram[b:b + 2].rearrange("b p d -> p b d")).then_inc(ld_x[b // 2], 16)
        sp.dma_start(ident[:, :], const["ident"]).then_inc(ld_c, 16)
        sp.dma_start(cos[:, :], const["cos"]).then_inc(ld_c, 16)
        sp.dma_start(sin[:, :], const["sin"]).then_inc(ld_c, 16)
        sp.dma_start(decay[:, :], const["causal"]).then_inc(ld_c, 16)
        sp.dma_start(square[0:3 * NH, 0:NH], const["pick"]).then_inc(ld_c, 16)
        sp.dma_start(gnorm[:, 0:1], w["gnorm"]).then_inc(ld_c, 16)
        sp.dma_start(head_col[:, 0:1], w["dt_bias"]).then_inc(ld_c, 16)
        sp.dma_start(head_col[:, 1:2], w["A_log"]).then_inc(ld_c, 16)
        sp.dma_start(win_raw, w["Win"]).then_inc(ld_dt, 16)
        sp.dma_start(raw_a[:, :, 0:HALF], w["Wv"][0]).then_inc(ld_v0, 16)
        sp.wait_ge(dve_win, KT)
        sp.dma_start(raw_b[:, :, :], w["Wv"][1]).then_inc(ld_v1, 16)
        sp.wait_ge(dve_wv, KT)
        sp.dma_start(raw_a[:, :, :], w["Wqk"][0]).then_inc(ld_qk, 16)
        sp.wait_ge(dve_wv, 2 * KT)
        sp.dma_start(raw_b[:, :, :], w["Wg"][0]).then_inc(ld_g, 16)

        def group(g, last):
            sp.wait_ge(dve_wqk, KT * g + KT)
            sp.dma_start(raw_a[:, :, 0:HALF], w["Wo"][bass.ds(g, 1)].rearrange("g p k n -> p (g k) n")).then_inc(ld_o, 16)
            if last:
                sp.wait_ge(dve_wg, KT * NG)
                sp.dma_start(raw_b[:, :, :], context[0]).then_inc(ld_ctx0, 16)
                sp.wait_ge(dve_wo, KT * NG)
                sp.dma_start(raw_a[:, :, 0:HALF], w["Xk"][0]).then_inc(ld_wk, 16)
            else:
                sp.wait_ge(dve_wg, KT * g + KT)
                sp.dma_start(raw_b[:, :, :], w["Wg"][bass.ds(g + 1, 1)].rearrange("g p k n -> p (g k) n")).then_inc(ld_g, 16)
                sp.wait_ge(dve_wo, KT * g + KT)
                sp.dma_start(raw_a[:, :, :], w["Wqk"][bass.ds(g + 1, 1)].rearrange("g p k n -> p (g k) n")).then_inc(ld_qk, 16)

        with sp.Fori(0, NG - 1) as g:
            group(g, False)
        group(NG - 1, True)

    @block.gpsimd
    def _(pool):
        def sine(g, t):
            pool.wait_ge(act_turn, TILES_QK * g + t + 1)
            tile = turned_q[:, t % 2, :].rearrange("p (b s) -> p b s", b=BPH)
            pool.tensor_tensor(tile, tile, sin[:, :].unsqueeze(1).broadcast_to([P, BPH, P]),
                               ALU.mult).then_inc(pool_sin, 1)

        def normalise_z(g, b):
            s = NB * g + b
            guess, t, minus_half, three_halves = (ssq[:, i, :] for i in (3, 4, 5, 6))
            pool.wait_ge(dve_ssq, 5 * s + 5)
            for i in range(NEWTON):
                step = 4 * NEWTON * s + 4 * i
                pool.tensor_tensor(t, guess, guess, ALU.mult).then_inc(pool_newton, 1)
                pool.wait_ge(pool_newton, step + 1)
                pool.tensor_tensor(t, t, minus_half, ALU.mult).then_inc(pool_newton, 1)
                pool.wait_ge(pool_newton, step + 2)
                pool.tensor_tensor(t, t, three_halves, ALU.add).then_inc(pool_newton, 1)
                pool.wait_ge(pool_newton, step + 3)
                pool.tensor_tensor(guess, guess, t, ALU.mult).then_inc(pool_newton, 1)
                pool.wait_ge(pool_newton, step + 4)
            pool.wait_ge(dve_z, s + 1)
            pool.tensor_tensor(heads(z[:, b % 2, :]), heads(z[:, b % 2, :]), per_head(guess),
                               ALU.mult).then_inc(pool_z, 1)

        def group(g, first):
            for t in range(FIRST_TILES):
                sine(g, t)
                if t == 1 and not first:
                    normalise_z(g - 1, NB - 1)
            for b in range(NB):
                for t in STEP_TILES.get(b, ()):
                    sine(g, t)
                if b >= 1:
                    normalise_z(g, b - 1)

        pool.memset(ssq[:, 6, :], 1.5).then_inc(zero_ready, 1)
        for part in win:
            pool.memset(part[:, :, NH:P].bitcast(F32), 0.0).then_inc(zero_ready, 1)
        pool.wait_ge(ld_c, 16 * 8)
        pool.wait_ge(zero_ready, 3)
        group(0, True)
        with pool.Fori(1, NG) as g:
            group(g, False)
        normalise_z(NG - 1, NB - 1)

    @block.scalar
    def _(act):
        norm_scalar_std(act, n)
        act.wait_ge(ld_dt, 16)
        for k in range(KT):
            act.activation(win[0][:, k, 0:NH], win_raw[:, k, :], ACT.Copy).then_inc(act_win, 1)
        for b in range(NB):
            act.wait_ge(n.turned, b + 1)
            act.activation(act_h[:, :, b * P:(b + 1) * P], heads(norm_banks[b % 4][:, :]),
                           ACT.Copy).then_inc(n.high_ready, 1)
        act.wait_ge(ld_v0, 16)
        for k in range(KT):
            act.activation(wg[0][:, k, :], raw_a[:, k, 0:HALF], ACT.Copy).then_inc(act_wv, 1)
        act.wait_ge(ld_v1, 16)
        for k in range(KT):
            act.activation(wo[0][:, k, :], raw_b[:, k, :], ACT.Copy).then_inc(act_wv, 1)

        def evacuate_v(i):
            act.wait_ge(pe_v, i + 1)
            act.activation(v_tok[:, i // 2, (i % 2) * HALF:(i % 2 + 1) * HALF], proj[i % RING][:, :],
                           ACT.Copy).then_inc(act_v, 1)

        act.wait_ge(ld_c, 16 * 8)
        act.activation(head_col[:, 2:3], head_col[:, 1:2], ACT.Exp).then_inc(act_dt, 1)
        evacuate_v(0)
        act.wait_ge(dt_step, 4)
        act.activation(e_row, e_row, ACT.Exp).then_inc(act_dt, 1)
        act.wait_ge(act_dt, 2)
        act.activation(e_row, e_row, ACT.Ln, bias=1.0).then_inc(act_dt, 1)
        evacuate_v(1)
        act.wait_ge(dt_step, 7)
        act.activation(t_rows, k_rows, ACT.Ln).then_inc(act_dt, 1)
        for i in range(2, NB):
            evacuate_v(i)

        def split_qk(g, k, first):
            if k == 0:
                act.wait_ge(ld_qk, 16 * g + 16)
                if first:
                    act.wait_ge(pe_dt, 2)
                else:
                    act.wait_ge(pe_qk, TILES_QK * g)
            act.activation(wqk[0][:, k, :], raw_a[:, k, :], ACT.Copy).then_inc(act_wqk, 1)

        def split_g(g, k, first):
            if k == 0:
                act.wait_ge(ld_g, 16 * g + 16)
                if first:
                    act.wait_ge(pe_v, 2 * NB)
                else:
                    act.wait_ge(pe_g, NB * g)
            act.activation(wg[0][:, k, :], raw_b[:, k, :], ACT.Copy).then_inc(act_wg, 1)

        def split_o(g, k, first):
            if k == 0:
                act.wait_ge(ld_o, 16 * g + 16)
                if first:
                    act.wait_ge(pe_v, 2 * NB)
                else:
                    act.wait_ge(pe_o, NB * g)
            act.activation(wo[0][:, k, :], raw_a[:, k, 0:HALF], ACT.Copy, scale=gnorm[:, 1:2]).then_inc(act_wo, 1)

        def turn(g, t, first):
            act.wait_ge(dve_cos, TILES_QK * g + t + 1)
            if t >= 2 or not first:
                act.wait_ge(dve_rope, TILES_QK * g + t - 1)
            src = ring_bank("qk", t)
            act.activation(turned_q[0:64, t % 2, :], src[64:128, :], ACT.Copy)
            act.activation(turned_q[64:128, t % 2, :], src[0:64, :], ACT.Copy).then_inc(act_turn, 1)

        def square_y(g, b):
            s = NB * g + b
            act.wait_ge(pe_y, s + 1)
            if later(g, b):
                act.wait_ge(dve_ssq, 5 * s - 4)
            act.activation(square[:, :], ps_y[:, :], ACT.Square).then_inc(act_square, 1)

        def high_z(g, b):
            s = NB * g + b
            act.wait_ge(pe_t, s + 1)
            if later(g, b):
                act.wait_ge(pe_o, s)
            act.activation(zt[0][:, :], ps_t[:, :], ACT.Copy).then_inc(act_zt, 1)

        def gate_tanh(g, b):
            s = NB * g + b
            act.wait_ge(pe_g, s + 1)
            if later(g, b):
                act.wait_ge(dve_gate, s)
            act.activation(tanh[:, :], ring_bank("gate", b)[:, :], ACT.Tanh, scale=0.5).then_inc(act_tanh, 1)

        def exp_decay(g, b):
            s = NB * g + b
            act.wait_ge(pe_d, s + 1)
            if later(g, b):
                act.wait_ge(dve_prob, s)
            if not later(g, b):
                act.wait_ge(bias_ready, 1)
            for h in range(HPG):
                mm = act.activation(decay[:, h * P:(h + 1) * P], ps_d[:, h * P:(h + 1) * P], ACT.Exp,
                                    bias=bias[:, b, bass.ds(g * HPG + h, 1)])
            mm.then_inc(act_decay, 1)

        def group(g, first, last):
            for t in range(FIRST_TILES):
                if t == 0 and not first:
                    high_z(g - 1, NB - 3)
                if t < KT:
                    split_g(g, t, first)
                turn(g, t, first)
                if t == 1 and not first:
                    square_y(g - 1, NB - 1)
                    high_z(g - 1, NB - 2)
                if t == 4 and not first:
                    high_z(g - 1, NB - 1)
            for b in range(NB):
                if b >= 3:
                    high_z(g, b - 3)
                gate_tanh(g, b)
                exp_decay(g, b)
                if b >= 1:
                    square_y(g, b - 1)
                for t in STEP_TILES.get(b, ()):
                    turn(g, t, first)
                if b in (1, 2):
                    split_o(g, 2 * b - 2, first)
                    split_o(g, 2 * b - 1, first)
                if not last:
                    for k in STEP_SPLITS.get(b, ()):
                        split_qk(g + 1, k, False)

        for k in range(KT):
            split_qk(0, k, True)
        for i in range(NB, 2 * NB):
            evacuate_v(i)
        group(0, True, False)
        with act.Fori(1, NG - 1) as g:
            group(g, False, False)
        group(NG - 1, False, True)
        high_z(NG - 1, NB - 3)
        square_y(NG - 1, NB - 1)
        high_z(NG - 1, NB - 2)
        high_z(NG - 1, NB - 1)

    @block.vector
    def _(dve):
        for b in range(NB):
            if b % 2 == 0:
                dve.wait_ge(ld_x[b // 2], 16)
            norm_block_stats(dve, n, x_res, b)
        norm_vector_rstd(dve, n)
        for b in range(NB):
            dve.tensor_scalar(xn[:, b, :], x_res[:, b, :], n.mv[:, b, 0:1], n.rs[:, b:b + 1],
                              ALU.subtract, ALU.mult).then_inc(n.xn_ready, 1)
        for k in range(KT):
            dve.wait_ge(act_win, k + 1)
            dve.tensor_tensor(win[1][:, k, 0:NH], win_raw[:, k, :], win[0][:, k, 0:NH].bitcast(F32),
                              ALU.subtract).then_inc(dve_win, 1)
        dve.wait_ge(ld_c, 16 * 8)
        dve.tensor_copy(causal[:, :], decay[:, :]).then_inc(const_ready, 1)
        dve.tensor_copy(ident_b[:, :], ident[:, :]).then_inc(const_ready, 1)
        dve.tensor_copy(pick[:, :], square[0:3 * NH, 0:NH]).then_inc(const_ready, 1)
        dve.tensor_scalar(gnorm[:, 1:2], gnorm[:, 0:1], 0.5, None, ALU.mult).then_inc(const_ready, 1)
        for b in range(NB):
            dve.wait_ge(n.high_ready, b + 1)
            cols = slice(b * P, (b + 1) * P)
            dve.tensor_tensor(act_l[:, :, cols], heads(norm_banks[b % 4][:, :]),
                              act_h[:, :, cols].bitcast(F32), ALU.subtract).then_inc(n.low_ready, 1)
        for i in range(2 * KT):
            part, raw, k = (wg, raw_a, i) if i < KT else (wo, raw_b, i - KT)
            dve.wait_ge(act_wv, i + 1)
            dve.tensor_tensor(part[1][:, k, :], raw[:, k, 0:HALF], part[0][:, k, :].bitcast(F32),
                              ALU.subtract).then_inc(dve_wv, 1)

        dve.wait_ge(pe_dt, 2)
        for half, bank in enumerate((ps_d, ps_y)):
            dve.tensor_scalar(z_row[:, half * HALF:(half + 1) * HALF], bank[0:NH, :], head_col[:, 0:1], None,
                              ALU.add).then_inc(dt_step, 1)
        dve.wait_ge(dt_step, 2)
        dve.scalar_tensor_tensor(out=e_row, in0=z_row, scalar=-1.0, in1=z_row, op0=ALU.mult,
                                 op1=ALU.min).then_inc(dt_step, 1)
        dve.tensor_scalar(dt_row, z_row, 0.0, None, ALU.max).then_inc(dt_step, 1)
        dve.wait_ge(dt_step, 4)
        dve.wait_ge(act_dt, 3)
        dve.tensor_tensor(dt_row, dt_row, e_row, ALU.add).then_inc(dt_step, 1)
        dve.tensor_scalar(head_col[:, 3:4], head_col[:, 2:3], -1.0, None, ALU.mult).then_inc(dt_step, 1)
        dve.wait_ge(dt_step, 6)
        dve.tensor_scalar(k_rows, dt_row, 1e-37, None, ALU.max).then_inc(dt_step, 1)
        dve.tensor_scalar(z_row, dt_row, head_col[:, 3:4], None, ALU.mult).then_inc(dt_step, 1)
        dve.memset(e_row, 1.0).then_inc(dt_step, 1)
        dve.wait_ge(dt_step, 9)
        for b in range(NB):
            dve.tensor_tensor_scan(cum_row[:, b * P:(b + 1) * P], e_row[:, b * P:(b + 1) * P],
                                   z_row[:, b * P:(b + 1) * P], 0.0, ALU.mult, ALU.add).then_inc(dt_step, 1)
        dve.wait_ge(dt_step, 9 + NB)
        dve.wait_ge(act_dt, 4)
        dve.tensor_tensor(dt_row, t_rows, cum_row, ALU.subtract).then_inc(dt_step, 1)
        count = 10 + NB
        for i in range(3):
            dve.wait_ge(dt_step, count)
            dve.tensor_copy(piece, cum_row).then_inc(dt_step, 1)
            count += 1
            dve.wait_ge(dt_step, count)
            dve.tensor_copy(cum3[i * NH:(i + 1) * NH, :], piece).then_inc(dt_step, 1)
            count += 1
            if i < 2:
                dve.tensor_tensor(cum_row, cum_row, piece, ALU.subtract).then_inc(dt_step, 1)
                count += 1
        assert count == DT_STEPS

        def low_qk(g, k):
            dve.wait_ge(act_wqk, KT * g + k + 1)
            dve.tensor_tensor(wqk[1][:, k, :], raw_a[:, k, :], wqk[0][:, k, :].bitcast(F32),
                              ALU.subtract).then_inc(dve_wqk, 1)

        def low_g(g, k):
            dve.wait_ge(act_wg, KT * g + k + 1)
            dve.tensor_tensor(wg[1][:, k, :], raw_b[:, k, :], wg[0][:, k, :].bitcast(F32),
                              ALU.subtract).then_inc(dve_wg, 1)

        def low_o(g, k):
            dve.wait_ge(act_wo, KT * g + k + 1)
            dve.scalar_tensor_tensor(out=wo[1][:, k, :], in0=raw_a[:, k, 0:HALF], scalar=gnorm[:, 1:2],
                                     in1=wo[0][:, k, :].bitcast(F32), op0=ALU.mult,
                                     op1=ALU.subtract).then_inc(dve_wo, 1)

        def rope_tile(t):
            half, j = t // FIRST_TILES, t % FIRST_TILES
            return (k_t[:, half, :] if j == 0 else q_t[:, half, j - 1, :]).rearrange("p (b s) -> p b s", b=BPH)

        def cosine(g, t, first):
            dve.wait_ge(pe_qk, TILES_QK * g + t + 1)
            if not first:
                if t == 0:
                    dve.wait_ge(pe_s, NB * g - BPH)
                if t == FIRST_TILES:
                    dve.wait_ge(pe_s, NB * g)
            dve.tensor_tensor(rope_tile(t), ring_bank("qk", t)[:, :].rearrange("p (b s) -> p b s", b=BPH),
                              cos[:, :].unsqueeze(1).broadcast_to([P, BPH, P]), ALU.mult).then_inc(dve_cos, 1)

        def add_sine(g, t):
            dve.wait_ge(pool_sin, TILES_QK * g + t + 1)
            dve.wait_ge(dve_cos, TILES_QK * g + t + 1)
            dve.tensor_tensor(rope_tile(t), rope_tile(t),
                              turned_q[:, t % 2, :].rearrange("p (b s) -> p b s", b=BPH),
                              ALU.add).then_inc(dve_rope, 1)

        def gate_silu(g, b):
            s = NB * g + b
            dve.wait_ge(act_tanh, s + 1)
            if later(g, b, 2):
                dve.wait_ge(dve_z, s - 1)
            dve.scalar_tensor_tensor(out=gate[:, b % 2, :], in0=tanh[:, :], scalar=1.0,
                                     in1=ring_bank("gate", b)[:, :], op0=ALU.add,
                                     op1=ALU.mult).then_inc(dve_gate, 1)

        def decayed(g, b):
            s = NB * g + b
            dve.wait_ge(act_decay, s + 1)
            dve.wait_ge(pe_s, s + 1)
            if later(g, b, 2):
                dve.wait_ge(pe_y, s - 1)
            dve.tensor_tensor(prob[:, b % 2, :], ps_s[:, :], decay[:, :], ALU.mult).then_inc(dve_prob, 1)

        def mean_square(g, b):
            s = NB * g + b
            total, mean, shifted, guess, minus_half = (ssq[:, i, :] for i in (0, 1, 2, 3, 5))
            dve.wait_ge(act_square, s + 1)
            dve.tensor_reduce(total, heads(square[:, :]), AX_X, ALU.add).then_inc(dve_ssq, 1)
            dve.wait_ge(dve_ssq, 5 * s + 1)
            if later(g, b):
                dve.wait_ge(pool_z, s)
            dve.tensor_scalar(mean, total, 1.0 / P, EPS, ALU.mult, ALU.add).then_inc(dve_ssq, 1)
            dve.tensor_scalar(minus_half, total, -0.5 / P, -0.5 * EPS, ALU.mult, ALU.add).then_inc(dve_ssq, 1)
            dve.wait_ge(dve_ssq, 5 * s + 2)
            dve.tensor_scalar(shifted.bitcast(I32), mean.bitcast(I32), 1, None,
                              ALU.logical_shift_right).then_inc(dve_ssq, 1)
            dve.wait_ge(dve_ssq, 5 * s + 4)
            dve.tensor_scalar(guess.bitcast(I32), shifted.bitcast(I32), -1, RSQRT_MAGIC, ALU.mult,
                              ALU.add).then_inc(dve_ssq, 1)

        def gated(g, b):
            s = NB * g + b
            dve.wait_ge(act_square, s + 1)
            if later(g, b, 2):
                dve.wait_ge(pe_t, s - 1)
            dve.tensor_tensor(z[:, b % 2, :], ps_y[:, :], gate[:, b % 2, :], ALU.mult).then_inc(dve_z, 1)

        def low_z(g, b):
            s = NB * g + b
            dve.wait_ge(act_zt, s + 1)
            dve.tensor_tensor(zt[1][:, :], ps_t[:, :], zt[0][:, :].bitcast(F32), ALU.subtract).then_inc(dve_zt, 1)

        def next_stats(b):
            dve.wait_ge(dve_acc, NB * (NG - 1) + b + 1)
            norm_block_stats(dve, next_norm, x_res, b)

        def accumulate(g, b, stats=True):
            s = NB * g + b
            dve.wait_ge(pe_o, s + 1)
            if later(g, b):
                dve.wait_ge(dve_acc, s)
            dve.tensor_tensor(x_res[:, b, :], x_res[:, b, :], ps_o[:, :], ALU.add).then_inc(dve_acc, 1)
            if isinstance(g, int) and g == NG - 1 and stats:
                next_stats(b)

        def group(g, first, last):
            for t in range(FIRST_TILES):
                if t == 0 and not first:
                    low_z(g - 1, NB - 3)
                cosine(g, t, first)
                if t >= 1:
                    add_sine(g, t - 1)
                if t < KT:
                    low_g(g, t)
                if not first:
                    if t == 1:
                        accumulate(g - 1, NB - 3)
                        gated(g - 1, NB - 1)
                        mean_square(g - 1, NB - 1)
                        low_z(g - 1, NB - 2)
                    if t == 4:
                        accumulate(g - 1, NB - 2)
            add_sine(g, FIRST_TILES - 1)
            if not first:
                low_z(g - 1, NB - 1)
            for b in range(NB):
                tiles = STEP_TILES.get(b, ())
                if b >= 3:
                    low_z(g, b - 3)
                gate_silu(g, b)
                decayed(g, b)
                if b >= 1:
                    gated(g, b - 1)
                    mean_square(g, b - 1)
                for t in tiles:
                    cosine(g, t, first)
                    if t != tiles[0]:
                        add_sine(g, t - 1)
                if b == 0 and not first:
                    accumulate(g - 1, NB - 1)
                if b in (1, 2):
                    low_o(g, 2 * b - 2)
                    low_o(g, 2 * b - 1)
                if b >= 3:
                    accumulate(g, b - 3)
                if not last:
                    for k in STEP_SPLITS.get(b, ()):
                        low_qk(g + 1, k)
                if tiles:
                    add_sine(g, tiles[-1])

        for k in range(KT):
            low_qk(0, k)
        dve.wait_ge(pe_bias, 1)
        dve.tensor_copy(bias[:, :, :], ps_d[:, 0:NB * NH].rearrange("p (b h) -> p b h", b=NB)).then_inc(bias_ready, 1)
        group(0, True, False)
        with dve.Fori(1, NG - 1) as g:
            group(g, False, False)
        group(NG - 1, False, True)
        low_z(NG - 1, NB - 3)
        gated(NG - 1, NB - 1)
        mean_square(NG - 1, NB - 1)
        accumulate(NG - 1, NB - 3, False)
        low_z(NG - 1, NB - 2)
        next_stats(NB - 3)
        accumulate(NG - 1, NB - 2)
        low_z(NG - 1, NB - 1)
        accumulate(NG - 1, NB - 1)

    @block.tensor
    def _(pe):
        pe.wait_ge(ld_c, 16 * 8)
        norm_tensor_turn(pe, n, xn, ident, norm_banks)
        pe.wait_ge(dve_win, KT)
        pe.wait_ge(zero_ready, 3)
        for half, bank in enumerate((ps_d, ps_y)):
            pe.wait_ge(n.low_ready, (half + 1) * BPH)
            pe.wait_ge(n.high_ready, (half + 1) * BPH)
            toks = slice(half * HALF, (half + 1) * HALF)
            for k in range(KT):
                mm = product3(pe, bank[:, :], [s[:, k, :] for s in win], (act_h[:, k, toks], act_l[:, k, toks]),
                              k == 0, k == KT - 1)
            mm.then_inc(pe_dt, 1)
        for i in range(2 * NB):
            b, part = i // 2, i % 2
            pe.wait_ge(dve_wv, KT * (part + 1))
            if i >= RING:
                pe.wait_ge(act_v, i - RING + 1)
            for k in range(KT):
                wv = (wg, wo)[part]
                mm = product3(pe, proj[i % RING][:, :],
                              (act_h[:, k, b * P:(b + 1) * P], act_l[:, k, b * P:(b + 1) * P]),
                              (wv[0][:, k, :], wv[1][:, k, :]), k == 0, k == KT - 1)
            mm.then_inc(pe_v, 1)

        def bank_free(g, kind, i, first):
            place = order.index((kind, i)) - RING
            if place < 0:
                if first:
                    return
                g = g - 1
            kind, i = order[place]
            if kind == "qk":
                pe.wait_ge(act_turn, TILES_QK * g + i + 1)
            else:
                pe.wait_ge(dve_gate, NB * g + i + 1)

        def qk_tile(g, t, first):
            half, j = t // FIRST_TILES, t % FIRST_TILES
            toks = slice(half * HALF, (half + 1) * HALF)
            if t == 0:
                pe.wait_ge(dve_wqk, KT * g + KT)
            bank_free(g, "qk", t, first)
            cols = slice(j * P, (j + 1) * P)
            for k in range(KT):
                mm = product3(pe, ring_bank("qk", t)[:, :], (wqk[0][:, k, cols], wqk[1][:, k, cols]),
                              (act_h[:, k, toks], act_l[:, k, toks]), k == 0, k == KT - 1)
            mm.then_inc(pe_qk, 1)

        def gate_tile(g, b):
            if b == 0:
                pe.wait_ge(dve_wg, KT * g + KT)
            bank_free(g, "gate", b, False)
            toks = slice(b * P, (b + 1) * P)
            for k in range(KT):
                mm = product3(pe, ring_bank("gate", b)[:, :], (act_h[:, k, toks], act_l[:, k, toks]),
                              (wg[0][:, k, :], wg[1][:, k, :]), k == 0, k == KT - 1)
            mm.then_inc(pe_g, 1)

        def decay_logs(g, b):
            s = NB * g + b
            if later(g, b):
                pe.wait_ge(act_decay, s)
            else:
                pe.wait_ge(bias_ready, 1)
            toks = slice(b * P, (b + 1) * P)
            pe.matmul(ps_d[:, :], ident_b[:, :], causal[:, :], start=True, stop=False, skip_group_check=True)
            for h in range(HPG):
                mm = pe.matmul(ps_d[:, h * P:(h + 1) * P],
                               pick[:, bass.ds(g * HPG + h, 1)].broadcast_to([3 * NH, P]), cum3[:, toks],
                               start=False, stop=h == HPG - 1, skip_group_check=True)
            mm.then_inc(pe_d, 1)

        def scores(g, b):
            s = NB * g + b
            if b % BPH == 0:
                pe.wait_ge(dve_rope, TILES_QK * g + (b // BPH + 1) * FIRST_TILES)
            if later(g, b):
                pe.wait_ge(dve_prob, s)
            half, toks = b // BPH, slice((b % BPH) * P, (b % BPH + 1) * P)
            pe.matmul(ps_s[:, :], k_t[:, half, toks], q_t[:, half, :, toks], start=True, stop=True).then_inc(pe_s, 1)

        def out_y(g, b):
            s = NB * g + b
            pe.wait_ge(dve_prob, s + 1)
            if later(g, b):
                pe.wait_ge(dve_z, s)
            for h in range(HPG):
                mm = pe.matmul(ps_y[:, h * P:(h + 1) * P], prob[:, b % 2, h * P:(h + 1) * P],
                               v_tok[:, b, bass.ds(g * P, P)], start=True, stop=True)
            mm.then_inc(pe_y, 1)

        def turn_z(g, b):
            s = NB * g + b
            pe.wait_ge(pool_z, s + 1)
            if later(g, b):
                pe.wait_ge(dve_zt, s)
            for h in range(HPG):
                mm = pe.transpose(ps_t[:, h * P:(h + 1) * P], z[:, b % 2, h * P:(h + 1) * P], ident[:, :])
            mm.then_inc(pe_t, 1)

        def project(g, b):
            s = NB * g + b
            if b == 0:
                pe.wait_ge(dve_wo, KT * g + KT)
            pe.wait_ge(dve_zt, s + 1)
            if later(g, b):
                pe.wait_ge(dve_acc, s)
            for h in range(HPG):
                cols = slice(h * P, (h + 1) * P)
                mm = product3(pe, ps_o[:, :], (zt[0][:, cols], zt[1][:, cols]), (wo[0][:, h, :], wo[1][:, h, :]),
                              h == 0, h == HPG - 1)
            mm.then_inc(pe_o, 1)

        def group(g, first):
            for t in range(FIRST_TILES):
                qk_tile(g, t, first)
                if t == 1 and not first:
                    project(g - 1, NB - 3)
                    out_y(g - 1, NB - 1)
                    turn_z(g - 1, NB - 2)
                if t == 4 and not first:
                    project(g - 1, NB - 2)
                    turn_z(g - 1, NB - 1)
            for b in range(NB):
                gate_tile(g, b)
                decay_logs(g, b)
                scores(g, b)
                if b >= 1:
                    out_y(g, b - 1)
                for t in STEP_TILES.get(b, ()):
                    qk_tile(g, t, first)
                if b == 0 and not first:
                    project(g - 1, NB - 1)
                if b >= 3:
                    project(g, b - 3)
                if b >= 2:
                    turn_z(g, b - 2)

        pe.wait_ge(act_v, 2 * NB)
        pe.wait_ge(const_ready, 4)
        pe.wait_ge(dt_step, DT_STEPS)
        for b in range(NB):
            mm = pe.transpose(ps_d[:, b * NH:(b + 1) * NH], dt_row[:, b * P:(b + 1) * P], ident[0:NH, 0:NH])
        mm.then_inc(pe_bias, 1)
        group(0, True)
        with pe.Fori(1, NG) as g:
            group(g, False)
        out_y(NG - 1, NB - 1)
        project(NG - 1, NB - 3)
        turn_z(NG - 1, NB - 2)
        project(NG - 1, NB - 2)
        turn_z(NG - 1, NB - 1)
        project(NG - 1, NB - 1)


def cross_attention(nc, ctx, x_res, act_h, act_l, ident, norms, raw_a, raw_b, ld_ctx0, ld_wk, ld_gu, const, w, context, mask):

    def sb(name, shape, dt):
        return ctx.enter_context(nc.sbuf_tensor(f"x_{name}", shape, dt))

    def sem(name):
        return ctx.enter_context(nc.semaphore(f"x_{name}"))

    def psum(name):
        return ctx.enter_context(nc.psum_tensor(f"x_ps_{name}", [P, 512], F32))

    wk, wq, wv, wo = ([sb(f"w{m}_{s}", [P, KT, HALF], F32R) for s in ("high", "low")] for m in "kqvo")
    ctx_h = sb("ctx_high", [P, KT, NB * P], F32R)
    ctx_l = sb("ctx_low", [P, KT, NB * P], F32R)
    ln_w = sb("ln_w", [P, KT], F32)
    bar = sb("bar", [P, NB, P], BF16)
    raw_a, pos = raw_a[:, :, 0:HALF], raw_a[:, :, HALF:HALF + P]
    kqv = sb("kqv", [P, 3 * HPG, HALF], F32)
    k_t, q_t, v_tok = (kqv[:, i * HPG:(i + 1) * HPG, :] for i in range(3))
    xn = kqv[:, HPG:HPG + NB, :]
    context1 = sb("context1", [P, KT, HALF], F32)
    mask_words = kqv[:, 0, 0:NB * P // 4].bitcast(I32).rearrange("p (b w) -> p b w", b=NB)
    pos_bar = sb("pos_bar", [P, HPG, P], F32)
    score, prob_t = context1[:, 0:3, :], context1[:, 3, :]
    at = [sb(f"at_{s}", [P, 2, HALF], F32R) for s in ("high", "low")]
    top, total, inverse = (sb(name, [P, HPG], F32) for name in ("top", "total", "inverse"))
    neg_top, row_sum = (sb(name, [P, 2, HPG], F32) for name in ("neg_top", "row_sum"))
    rms = sb("rms", [P, 3, NB], F32)

    proj = [psum(f"proj{i}") for i in range(RING)]
    ps_s, ps_t, ps_y, ps_o = (psum(s) for s in ("scores", "turn", "y", "out"))

    n, next_norm = norms
    norm_banks = [ps_t, ps_o, ps_s, ps_y]
    ld_c, ld_mask, ld_ctx1 = sem("ld_c"), sem("ld_mask"), sem("ld_ctx1")
    ld = {"k": ld_wk, **{m: sem(f"ld_w{m}") for m in "qvo"}}
    ld_pos = sem("ld_pos")
    act_w = {m: sem(f"act_w{m}") for m in "kqvo"}
    dve_w = {m: sem(f"dve_w{m}") for m in "kqvo"}
    weights = dict(k=wk, q=wq, v=wv, o=wo)
    raw = dict(k=raw_a, v=raw_a, q=raw_b, o=raw_b)
    act_ctx, pool_ctx, const_ready = sem("act_ctx"), sem("pool_ctx"), sem("const_ready")
    rms_step, rms_std, h_added = sem("rms_step"), sem("rms_std"), sem("h_added")
    pe_pr, act_pr = sem("pe_pr"), sem("act_pr")
    pe_s, pe_t, pe_y, pe_o = sem("pe_s"), sem("pe_t"), sem("pe_y"), sem("pe_o")
    dve_sum, dve_max, act_exp, dve_inv = sem("dve_sum"), sem("dve_max"), sem("act_exp"), sem("dve_inv")
    pool_bar = sem("pool_bar")
    pool_norm, dve_pt, act_at, dve_at, dve_acc = (sem("pool_norm"), sem("dve_pt"), sem("act_at"), sem("dve_at"),
                                                  sem("dve_acc"))
    TILES = 2 * HPG
    PER = TILES + BPH
    DRAIN = 4

    def parts(k):
        return [k - lag if 0 <= k - lag < BPH else None for lag in range(5)]

    def any_later(g, half, b, lag=1):
        return later(g, BPH * half + b, lag)

    block = ctx.enter_context(nc.Block())

    @block.sync
    def _(sp):
        sp.dma_start(ln_w[:, :], w["ln_w"]).then_inc(ld_c, 16)
        sp.dma_start(mask_words, mask).then_inc(ld_mask, 16)
        sp.wait_ge(pool_ctx, KT)
        sp.dma_start(raw_b[:, :, :], w["Xq"][0]).then_inc(ld["q"], 16)
        sp.dma_start(context1[:, :, :], context[1]).then_inc(ld_ctx1, 16)
        sp.dma_start(pos, w["pos"][0]).then_inc(ld_pos, 16)

        def load(m, g):
            sp.dma_start(raw[m][:, :, :], w[f"X{m}"][bass.ds(g, 1)].rearrange("g p k n -> p (g k) n")).then_inc(ld[m], 16)

        def group(g, last):
            sp.wait_ge(dve_w["q"], KT * g + KT)
            load("o", g)
            if last:
                for parity, m in enumerate("vo"):
                    sp.wait_ge(dve_w[m], KT * NG)
                    sp.dma_start((raw_a, raw_b)[parity][:, :, :], w["gu"][parity]).then_inc(ld_gu[parity], 16)
            else:
                sp.wait_ge(dve_w["v"], KT * g + KT)
                load("k", g + 1)
                sp.wait_ge(dve_w["o"], KT * g + KT)
                load("q", g + 1)
                sp.wait_ge(dve_w["k"], KT * g + 2 * KT)
                load("v", g + 1)
                sp.wait_ge(pool_bar, NB * g + NB)
                sp.dma_start(pos, w["pos"][bass.ds(g + 1, 1)].rearrange("g q h k -> q (g h) k")).then_inc(ld_pos, 16)

        sp.wait_ge(dve_w["k"], KT)
        load("v", 0)
        with sp.Fori(0, NG - 1) as g:
            group(g, False)
        group(NG - 1, True)

    @block.gpsimd
    def _(pool):
        def normalise(g, b):
            s = NB * g + b
            pool.wait_ge(dve_inv, 2 * s + 2)
            tile = heads(score[:, b % BPH % 3, :])
            pool.tensor_tensor(tile, tile, per_head(inverse[:, :]), ALU.mult).then_inc(pool_norm, 1)

        def bias_and_bar(g, half, b):
            s = NB * g + BPH * half + b
            if half == 0 and b == 0:
                pool.wait_ge(ld_pos, 16 * g + 16)
            if b >= 1:
                pool.wait_ge(dve_sum, s)
            pool.tensor_tensor(pos_bar[:, :, :], pos, bar[:, BPH * half + b, :].unsqueeze(1).broadcast_to([P, HPG, P]),
                               ALU.add).then_inc(pool_bar, 1)

        for half, raw_ctx in enumerate((raw_b, context1)):
            for k in range(KT):
                cols = slice(half * HALF, (half + 1) * HALF)
                pool.wait_ge(act_ctx, half * KT + k + 1)
                pool.tensor_tensor(ctx_l[:, k, cols], raw_ctx[:, k, :], ctx_h[:, k, cols].bitcast(F32),
                                   ALU.subtract).then_inc(pool_ctx, 1)
        pool.wait_ge(const_ready, 1)
        with pool.Fori(0, NG) as g:
            for half in range(2):
                for b in range(BPH + 2):
                    if b < BPH:
                        bias_and_bar(g, half, b)
                    if b >= 2:
                        normalise(g, BPH * half + b - 2)

    @block.scalar
    def _(act):
        def split_ctx(half, k):
            if k == 0:
                act.wait_ge((ld_ctx0, ld_ctx1)[half], 16)
            act.activation(ctx_h[:, k, half * HALF:(half + 1) * HALF], (raw_b, context1)[half][:, k, :],
                           ACT.Copy).then_inc(act_ctx, 1)

        def split(m, g, k, free):
            if k == 0:
                act.wait_ge(ld[m], 16 * g + 16)
                if free is not None:
                    act.wait_ge(*free)
            scale = ln_w[:, k:k + 1] if m == "q" else 1.0
            act.activation(weights[m][0][:, k, :], raw[m][:, k, :], ACT.Copy, scale=scale).then_inc(act_w[m], 1)

        def evacuate(g, half, t):
            u = 2 * g + half
            act.wait_ge(pe_pr, PER * u + t + 1)
            act.activation(kqv[:, t, :], proj[t % RING][:, :], ACT.Copy).then_inc(act_pr, 1)

        def step(g, half, k, last=True):
            scored, _, _, _, out = parts(k)
            s0 = NB * g + BPH * half
            if out is not None:
                act.wait_ge(pe_y, s0 + out + 1)
                if any_later(g, half, out, 2):
                    act.wait_ge(pe_o, s0 + out - 1)
                act.activation(at[0][:, out % 2, :], ps_y[:, :], ACT.Copy).then_inc(act_at, 1)
            if scored is not None:
                if isinstance(g, int) and s0 + scored == 0:
                    act.wait_ge(h_added, NB)
                evacuate(g, half, TILES + scored)
                if half == 0 and scored < 3:
                    split("o", g, scored + 1, None)
                if half == 1 and not last:
                    split("q", g + 1, scored, (pe_pr, PER * (2 * g + 1) + TILES))
                s = s0 + scored
                act.wait_ge(dve_max, 2 * s + 2)
                if any_later(g, half, scored, 2):
                    act.wait_ge(dve_inv, 2 * s - 2)
                tile = score[:, scored % 3, :]
                for h in range(HPG):
                    cols = slice(h * P, (h + 1) * P)
                    act.activation(tile[:, cols], tile[:, cols], ACT.Exp, bias=neg_top[:, scored % 2, h:h + 1],
                                   accum_out=row_sum[:, scored % 2, h:h + 1]).then_inc(act_exp, 1)

        def turned_high(blocks):
            for b in blocks:
                act.wait_ge(n.turned, b + 1)
                act.activation(act_h[:, :, b * P:(b + 1) * P], heads(norm_banks[b % 4][:, :]),
                               ACT.Copy).then_inc(n.high_ready, 1)

        def unit(g, half, first, last):
            for t in range(TILES):
                if t % 2 == 1 and not first:
                    step(*before(g, half), BPH + t // 2)
                if first and t == 0:
                    act.wait_ge(const_ready, 1)
                if first and t == HPG:
                    act.wait_ge(h_added, BPH)
                evacuate(g, half, t)
                if first and t == HPG - 1:
                    turned_high(range(BPH, NB))
                if first and HPG - 1 <= t < 2 * HPG - 1:
                    split_ctx(1, t - HPG + 1)
                if half == 0:
                    if t < KT:
                        split("v", g, t, None if first else (pe_pr, 2 * PER * g))
                    if t == TILES - 1:
                        split("o", g, 0, None if first else (pe_o, NB * g))
                elif t >= HPG and not last:
                    split("k", g + 1, t - HPG, (pe_pr, PER * (2 * g + 1) + HPG))
            for b in range(BPH):
                step(g, half, b, last)

        norm_scalar_std(act, n)
        for k in range(KT):
            split_ctx(0, k)
            if k == 1:
                act.wait_ge(rms_step, 3)
                act.activation(rms[:, 2, :], rms[:, 1, :], ACT.Sqrt).then_inc(rms_std, 1)
        for k in range(KT):
            split("k", 0, k, None)
        turned_high(range(BPH))
        act.wait_ge(ld_c, 16)
        for k in range(KT):
            split("q", 0, k, None)
        unit(0, 0, True, False)
        unit(0, 1, False, False)
        with act.Fori(1, NG - 1) as g:
            unit(g, 0, False, False)
            unit(g, 1, False, False)
        unit(NG - 1, 0, False, True)
        unit(NG - 1, 1, False, True)
        for k in range(BPH, BPH + DRAIN):
            step(NG - 1, 1, k)

    @block.vector
    def _(dve):
        norm_vector_rstd(dve, n)
        square, mean_square, root = (rms[:, i, :] for i in range(3))
        inverse_rms, scale = square, mean_square
        dve.tensor_tensor(square, n.rs[:, :], n.rs[:, :], ALU.mult).then_inc(rms_step, 1)
        dve.wait_ge(rms_step, 1)
        dve.tensor_tensor(square, square, n.mv[:, :, 1], ALU.mult).then_inc(rms_step, 1)
        dve.wait_ge(rms_step, 2)
        dve.tensor_scalar(mean_square, square, EPS, None, ALU.add).then_inc(rms_step, 1)
        dve.wait_ge(rms_std, 1)
        dve.reciprocal(inverse_rms, root).then_inc(rms_step, 1)
        dve.wait_ge(rms_step, 4)
        dve.tensor_tensor(scale, inverse_rms, n.rs[:, :], ALU.mult).then_inc(rms_step, 1)
        dve.wait_ge(rms_step, 5)

        def normalise(blocks):
            for b in blocks:
                dve.tensor_scalar(xn[:, b, :], x_res[:, b, :], n.mv[:, b, 0:1], scale[:, b:b + 1],
                                  ALU.subtract, ALU.mult).then_inc(n.xn_ready, 1)

        def turned_low(blocks):
            for b in blocks:
                dve.wait_ge(n.high_ready, b + 1)
                cols = slice(b * P, (b + 1) * P)
                dve.tensor_tensor(act_l[:, :, cols], heads(norm_banks[b % 4][:, :]),
                                  act_h[:, :, cols].bitcast(F32), ALU.subtract).then_inc(n.low_ready, 1)

        def add_h(blocks):
            for b in blocks:
                dve.scalar_tensor_tensor(out=x_res[:, b, :], in0=xn[:, b, :], scalar=rms[:, 2, b:b + 1],
                                         in1=x_res[:, b, :], op0=ALU.mult, op1=ALU.add).then_inc(h_added, 1)

        def low(m, g, k):
            dve.wait_ge(act_w[m], KT * g + k + 1)
            if m == "q":
                dve.scalar_tensor_tensor(out=wq[1][:, k, :], in0=raw_b[:, k, :], scalar=ln_w[:, k:k + 1],
                                         in1=wq[0][:, k, :].bitcast(F32), op0=ALU.mult,
                                         op1=ALU.subtract).then_inc(dve_w[m], 1)
            else:
                dve.tensor_tensor(weights[m][1][:, k, :], raw[m][:, k, :], weights[m][0][:, k, :].bitcast(F32),
                                  ALU.subtract).then_inc(dve_w[m], 1)

        def output_low(g, half, out):
            s = NB * g + BPH * half + out
            dve.wait_ge(act_at, s + 1)
            dve.tensor_tensor(at[1][:, out % 2, :], ps_y[:, :], at[0][:, out % 2, :].bitcast(F32),
                              ALU.subtract).then_inc(dve_at, 1)

        def invert(g, half, b):
            s = NB * g + BPH * half + b
            dve.wait_ge(act_exp, HPG * (s + 1))
            if any_later(g, half, b):
                dve.wait_ge(dve_inv, 2 * s)
            dve.tensor_scalar(total[:, :], row_sum[:, b % 2, :], 1e-30, None, ALU.max).then_inc(dve_inv, 1)
            dve.wait_ge(dve_inv, 2 * s + 1)
            if any_later(g, half, b):
                dve.wait_ge(pool_norm, s)
            dve.reciprocal(inverse[:, :], total[:, :]).then_inc(dve_inv, 1)

        def copy_turned(g, half, b):
            s = NB * g + BPH * half + b
            dve.wait_ge(pe_t, s + 1)
            if any_later(g, half, b):
                dve.wait_ge(pe_y, s)
            dve.tensor_copy(prob_t, ps_t[:, :]).then_inc(dve_pt, 1)

        def accumulate(g, half, out):
            s = NB * g + BPH * half + out
            b = BPH * half + out
            dve.wait_ge(pe_o, s + 1)
            if any_later(g, half, out):
                dve.wait_ge(dve_acc, s)
            else:
                dve.wait_ge(h_added, NB)
            dve.tensor_tensor(x_res[:, b, :], x_res[:, b, :], ps_o[:, :], ALU.add).then_inc(dve_acc, 1)
            if isinstance(g, int) and g == NG - 1:
                dve.wait_ge(dve_acc, s + 1)
                norm_block_stats(dve, next_norm, x_res, b)

        def step(g, half, k, last=True):
            scored, inverted, turned, _, out = parts(k)
            if out is not None:
                output_low(g, half, out)
            if k == 3:
                copy_turned(g, half, 0)
            if scored is not None:
                s0 = NB * g + BPH * half
                s = s0 + scored
                tile = score[:, scored % 3, :]
                dve.wait_ge(pe_s, s + 1)
                if isinstance(g, int) and s == 0:
                    dve.wait_ge(pool_ctx, 2 * KT)
                dve.wait_ge(pool_bar, s + 1)
                if scored == 3 or any_later(g, half, 0):
                    dve.wait_ge(pe_t, s0 + (1 if scored == 3 else 0))
                dve.tensor_tensor(heads(tile), heads(ps_s[:, :]), pos_bar[:, :, :], ALU.add).then_inc(dve_sum, 1)
                dve.wait_ge(dve_sum, s + 1)
                dve.tensor_reduce(top[:, :], heads(tile), AX_X, ALU.max).then_inc(dve_max, 1)
                dve.wait_ge(dve_max, 2 * s + 1)
                if any_later(g, half, scored, 2):
                    dve.wait_ge(act_exp, HPG * (s - 1))
                dve.tensor_scalar(neg_top[:, scored % 2, :], top[:, :], 0.1 * NEG, -1.0, ALU.max,
                                  ALU.mult).then_inc(dve_max, 1)
                if half == 0 and scored < 3:
                    low("o", g, scored + 1)
                if half == 1 and not last:
                    low("q", g + 1, scored)
            if inverted is not None:
                invert(g, half, inverted)
            if turned is not None and k >= 3:
                copy_turned(g, half, turned)
            if out is not None:
                accumulate(g, half, out)

        def unit(g, half, first, last):
            for t in range(TILES):
                if t % 2 == 1 and not first:
                    step(*before(g, half), BPH + t // 2)
                if first and t == HPG:
                    turned_low(range(BPH, NB))
                    add_h(range(BPH, NB))
                if half == 0:
                    if t < KT:
                        low("v", g, t)
                    if t == TILES - 1:
                        low("o", g, 0)
                elif t >= HPG and not last:
                    low("k", g + 1, t - HPG)
            for b in range(BPH):
                step(g, half, b, last)

        normalise(range(BPH))
        for k in range(KT):
            low("k", 0, k)
        normalise(range(BPH, NB))
        dve.wait_ge(ld_mask, 16)
        dve.tensor_scalar(bar[:, :, :], mask_words.bitcast(U8), -1.0, -NEG, ALU.add, ALU.mult).then_inc(const_ready, 1)
        turned_low(range(BPH))
        dve.wait_ge(n.xn_ready, NB)
        add_h(range(BPH))
        dve.wait_ge(ld_c, 16)
        for k in range(KT):
            low("q", 0, k)
        unit(0, 0, True, False)
        unit(0, 1, False, False)
        with dve.Fori(1, NG - 1) as g:
            unit(g, 0, False, False)
            unit(g, 1, False, False)
        unit(NG - 1, 0, False, True)
        unit(NG - 1, 1, False, True)
        output_low(NG - 1, 1, 0)
        invert(NG - 1, 1, 3)
        copy_turned(NG - 1, 1, 2)
        output_low(NG - 1, 1, 1)
        accumulate(NG - 1, 1, 0)
        copy_turned(NG - 1, 1, 3)
        output_low(NG - 1, 1, 2)
        accumulate(NG - 1, 1, 1)
        output_low(NG - 1, 1, 3)
        accumulate(NG - 1, 1, 2)
        accumulate(NG - 1, 1, 3)


    @block.tensor
    def _(pe):
        norm_tensor_turn(pe, n, xn, ident, norm_banks, range(BPH))
        pe.wait_ge(pool_ctx, KT)

        def ring_free(g, half, t):
            u = 2 * g + half
            if half or t >= RING or not isinstance(g, int) or g > 0:
                pe.wait_ge(act_pr, PER * u + t - RING + 1)

        def tile(g, half, t):
            j = t % HPG
            m, rhs = ("k", (ctx_h, ctx_l)) if t < HPG else ("q", (act_h, act_l))
            wm = weights[m]
            if half == 0 and j == 0:
                pe.wait_ge(dve_w[m], KT * g + KT)
            if isinstance(g, int) and g == 0 and t == (0 if half else HPG):
                pe.wait_ge(n.low_ready, (half + 1) * BPH)
                pe.wait_ge(n.high_ready, (half + 1) * BPH)
                if half:
                    pe.wait_ge(pool_ctx, 2 * KT)
            ring_free(g, half, t)
            toks, cols = slice(half * HALF, (half + 1) * HALF), slice(j * P, (j + 1) * P)
            for k in range(KT):
                mm = product3(pe, proj[t % RING][:, :], (wm[0][:, k, cols], wm[1][:, k, cols]),
                              (rhs[0][:, k, toks], rhs[1][:, k, toks]), k == 0, k == KT - 1)
            mm.then_inc(pe_pr, 1)

        def v_tile(g, half, b):
            if half == 0 and b == 0:
                pe.wait_ge(dve_w["v"], KT * g + KT)
            ring_free(g, half, TILES + b)
            toks = slice((BPH * half + b) * P, (BPH * half + b + 1) * P)
            for k in range(KT):
                mm = product3(pe, proj[(TILES + b) % RING][:, :], (ctx_h[:, k, toks], ctx_l[:, k, toks]),
                              (wv[0][:, k, :], wv[1][:, k, :]), k == 0, k == KT - 1)
            mm.then_inc(pe_pr, 1)

        def turn(g, half, turned):
            s = NB * g + BPH * half + turned
            pe.wait_ge(pool_norm, s + 1)
            if any_later(g, half, turned):
                pe.wait_ge(dve_pt, s)
            for h in range(HPG):
                cols = slice(h * P, (h + 1) * P)
                mm = pe.transpose(ps_t[:, cols], score[:, turned % 3, cols], ident[:, :])
            mm.then_inc(pe_t, 1)

        def mix(g, half, mixed):
            u, s = 2 * g + half, NB * g + BPH * half + mixed
            pe.wait_ge(dve_pt, s + 1)
            pe.wait_ge(act_pr, PER * u + TILES + mixed + 1)
            if any_later(g, half, mixed):
                pe.wait_ge(dve_at, s)
            for h in range(HPG):
                cols = slice(h * P, (h + 1) * P)
                mm = pe.matmul(ps_y[:, cols], v_tok[:, mixed, cols], prob_t[:, cols], start=True, stop=True)
            mm.then_inc(pe_y, 1)

        def step(g, half, k):
            scored, _, turned, mixed, out = parts(k)
            u, s0 = 2 * g + half, NB * g + BPH * half
            if scored is not None:
                s = s0 + scored
                v_tile(g, half, scored)
                if k == 3:
                    turn(g, half, 0)
                if isinstance(g, int) and s == 0:
                    pe.wait_ge(n.low_ready, NB)
                if scored == 0:
                    pe.wait_ge(act_pr, PER * u + TILES)
                if any_later(g, half, scored):
                    pe.wait_ge(dve_sum, s)
                toks = slice(scored * P, (scored + 1) * P)
                for h in range(HPG):
                    mm = pe.matmul(ps_s[:, h * P:(h + 1) * P], q_t[:, h, toks], k_t[:, h, toks], start=True, stop=True)
                mm.then_inc(pe_s, 1)
            if k == 3:
                mix(g, half, mixed)
            if turned is not None and k >= 3:
                turn(g, half, turned)
            if mixed is not None and k > 3:
                mix(g, half, mixed)
            if out is not None:
                s = s0 + out
                if half == 0 and out == 0:
                    pe.wait_ge(dve_w["o"], KT * g + KT)
                pe.wait_ge(dve_at, s + 1)
                if any_later(g, half, out):
                    pe.wait_ge(dve_acc, s)
                for h in range(HPG):
                    cols = slice(h * P, (h + 1) * P)
                    mm = product3(pe, ps_o[:, :], (at[0][:, out % 2, cols], at[1][:, out % 2, cols]), (wo[0][:, h, :], wo[1][:, h, :]),
                                  h == 0, h == HPG - 1)
                mm.then_inc(pe_o, 1)

        def unit(g, half, first):
            for t in range(TILES):
                if first and t == HPG:
                    norm_tensor_turn(pe, n, xn, ident, norm_banks, range(BPH, NB))
                tile(g, half, t)
                if t % 2 == 1 and not first:
                    step(*before(g, half), BPH + t // 2)
            for b in range(BPH):
                step(g, half, b)

        unit(0, 0, True)
        unit(0, 1, False)
        with pe.Fori(1, NG) as g:
            unit(g, 0, False)
            unit(g, 1, False)
        for k in range(BPH, BPH + DRAIN):
            step(NG - 1, 1, k)


def experts(nc, ctx, x_res, act_h, act_l, ident, n, raw_gu, ld_gu, const, w, out_dram):

    def sb(name, shape, dt):
        return ctx.enter_context(nc.sbuf_tensor(f"m_{name}", shape, dt))

    def sem(name):
        return ctx.enter_context(nc.semaphore(f"m_{name}"))

    def psum(name):
        return ctx.enter_context(nc.psum_tensor(f"m_ps_{name}", [P, 512], F32))

    PAIRS = NCOMB // 2
    raw_d = sb("raw_d", [P, 2, 2, HID], F32)
    wgu = [sb(f"wgu_{s}", [P, 2, KT, HALF], F32R) for s in ("high", "low")]
    wd = [sb(f"wd_{s}", [P, 2, 2, HID], F32R) for s in ("high", "low")]
    zt = [sb(f"z_{s}", [P, 2, 2, NB * P], F32R) for s in ("high", "low")]
    silu = sb("silu", [P, 2, HALF], F32)
    z = sb("z", [P, 2, HALF], F32)
    xn = sb("xn", [P, NB, HID], F32)
    router_raw = sb("router_raw", [P, KT, NEXP], F32)
    router = [sb(f"router_{s}", [P, KT, P], F32R) for s in ("high", "low")]
    logit_row = sb("logit_row", [NEXP, NB * P], F32)
    ident_b = sb("ident_b", [P, P], BF16)
    pick_raw = sb("pick_raw", [3 * NH, NH], F32)
    pick = sb("pick", [3 * NH, NH], BF16)
    order = sb("order", [P, NEXP], F32)
    logit, prob, rest, hit, first_hit, second_hit, weigh = (
        sb(s, [P, NB, NEXP], F32) for s in ("logit", "prob", "rest", "hit", "first_hit", "second_hit", "weigh"))
    col = sb("col", [P, 8, NB], F32)
    comb = sb("comb", [P, NB, NCOMB], F32)
    pieces = sb("pieces", [P, NB, 3 * NH], BF16)
    comb3 = sb("comb3", [3 * NH, NB * P], BF16)

    ps_g, ps_u = [psum("g0"), psum("g1")], [psum("u0"), psum("u1")]
    ps_c = psum("weight")
    ps_o = [psum("out0"), psum("out1")]

    norm_banks = ps_o + ps_g
    ld_c, ld_d = sem("ld_c"), [sem("ld_d0"), sem("ld_d1")]
    const_ready, act_router, dve_router = sem("const_ready"), sem("act_router"), sem("dve_router")
    pe_logit, dve_logit, pe_logit_turned = sem("pe_logit"), sem("dve_logit"), sem("pe_logit_turned")
    route, act_route, pe_comb, comb_ready = sem("route"), sem("act_route"), sem("pe_comb"), sem("comb_ready")
    act_gu, dve_gu, act_d, dve_d = sem("act_gu"), sem("dve_gu"), sem("act_d"), sem("dve_d")
    pe_g, pe_u, pe_c, pe_o = sem("pe_g"), sem("pe_u"), sem("pe_c"), sem("pe_o")
    act_silu, dve_weighed, dve_z, act_zh, pool_zl, dve_acc = (sem("act_silu"), sem("dve_weighed"), sem("dve_z"),
                                                              sem("act_zh"), sem("pool_zl"), sem("dve_acc"))
    zero_ready, stored = sem("zero_ready"), sem("stored")
    STEPS = 4

    def loops(eng, body):
        body(0, 0, True, False)
        body(1, 1, False, False)
        with eng.Fori(1, PAIRS // 2 - 1) as turn:
            body(2 * turn, 0, False, False)
            body(2 * turn + 1, 1, False, False)
        body(PAIRS - 2, 0, False, False)
        body(PAIRS - 1, 1, False, True)

    def at_start(p, j, lag=1):
        return isinstance(p, int) and STEPS * p + j < lag

    block = ctx.enter_context(nc.Block())

    @block.sync
    def _(sp):
        sp.dma_start(router_raw[:, :, :], w["router"]).then_inc(ld_c, 16)
        sp.dma_start(pick_raw[:, :], const["pick"]).then_inc(ld_c, 16)
        sp.dma_start(order[:, :], const["order"]).then_inc(ld_c, 16)

        def load(p, parity, wait):
            if wait:
                sp.wait_ge(dve_gu, KT * (p - 1))
                sp.dma_start(raw_gu[parity][:, :, :], w["gu"][bass.ds(p, 1)].rearrange("e p k n -> p (e k) n")).then_inc(ld_gu[parity], 16)
            if wait:
                sp.wait_ge(dve_d, 2 * (p - 1))
            sp.dma_start(raw_d[:, parity, :, :], w["down"][bass.ds(p, 1)].rearrange("e p k n -> p (e k) n")).then_inc(ld_d[parity], 16)

        load(0, 0, False)
        load(1, 1, False)
        with sp.Fori(1, PAIRS // 2) as turn:
            load(2 * turn, 0, True)
            load(2 * turn + 1, 1, True)
        for b in range(NB):
            sp.wait_ge(dve_acc, NB * (PAIRS - 1) + b + 1)
            sp.dma_start(out_dram[b], x_res[:, b, :]).then_inc(stored, 16)
        sp.wait_ge(stored, 16 * NB)

    @block.gpsimd
    def _(pool):
        for part in router:
            pool.memset(part[:, :, NEXP:P].bitcast(F32), 0.0).then_inc(zero_ready, 1)
        pool.memset(pieces[:, :, :], 0.0).then_inc(zero_ready, 1)
        pool.memset(comb[:, :, NEXP:NCOMB], 1.0).then_inc(zero_ready, 1)

        def body(p, parity, first, last):
            for j in range(STEPS):
                s = STEPS * p + j
                toks = slice((j % 2) * HALF, (j % 2 + 1) * HALF)
                pool.wait_ge(act_zh, s + 1)
                pool.tensor_tensor(zt[1][:, parity, j // 2, toks], z[:, j % 2, :],
                                   zt[0][:, parity, j // 2, toks].bitcast(F32), ALU.subtract).then_inc(pool_zl, 1)

        loops(pool, body)

    @block.scalar
    def _(act):
        def split_gu(p, parity, k):
            if k == 0:
                act.wait_ge(ld_gu[parity], load_count(p, parity))
                if not (isinstance(p, int) and p < 2):
                    act.wait_ge(pe_u, STEPS * (p - 1))
            act.activation(wgu[0][:, parity, k, :], raw_gu[parity][:, k, :], ACT.Copy).then_inc(act_gu, 1)

        def split_d(p, parity, k):
            if k == 0:
                act.wait_ge(ld_d[parity], load_count(p, parity))
                if not (isinstance(p, int) and p < 2):
                    act.wait_ge(pe_o, NB * (p - 1))
            act.activation(wd[0][:, parity, k, :], raw_d[:, parity, k, :], ACT.Copy).then_inc(act_d, 1)

        def load_count(p, parity):
            return 8 * p + 16 if parity == 0 else 8 * p + 8

        norm_scalar_std(act, n)
        act.wait_ge(ld_c, 48)
        act.activation(router[0][:, :, 0:NEXP], router_raw[:, :, :], ACT.Copy).then_inc(act_router, 1)
        for k in range(KT):
            split_gu(0, 0, k)
        for b in range(NB):
            act.wait_ge(n.turned, b + 1)
            act.activation(act_h[:, :, b * P:(b + 1) * P], heads(norm_banks[b % 4][:, :]),
                           ACT.Copy).then_inc(n.high_ready, 1)
        for k in range(KT):
            split_gu(1, 1, k)
        act.wait_ge(route, 3)
        act.activation(prob[:, :, :], rest[:, :, :], ACT.Exp).then_inc(act_route, 1)

        def high_z(p, parity, j):
            s = STEPS * p + j
            toks = slice((j % 2) * HALF, (j % 2 + 1) * HALF)
            act.wait_ge(dve_z, s + 1)
            if j == 0 and not (isinstance(p, int) and p < 2):
                act.wait_ge(pe_o, NB * (p - 1))
            act.activation(zt[0][:, parity, j // 2, toks], z[:, j % 2, :], ACT.Copy).then_inc(act_zh, 1)

        def body(p, parity, first, last):
            for j in range(STEPS):
                s = STEPS * p + j
                if j > 0:
                    high_z(p, parity, j - 1)
                elif not first:
                    high_z(p - 1, 1 - parity, STEPS - 1)
                act.wait_ge(pe_g, s + 1)
                if not at_start(p, j, 2):
                    act.wait_ge(dve_z, s - 1)
                act.activation(silu[:, j % 2, :], ps_g[j % 2][:, :], ACT.Silu).then_inc(act_silu, 1)
                if not (first or last):
                    split_gu(p + 1, 1 - parity, j)
                if j < 2:
                    split_d(p, parity, j)

        loops(act, body)
        high_z(PAIRS - 1, 1, STEPS - 1)

    @block.vector
    def _(dve):
        norm_vector_rstd(dve, n)
        for b in range(NB):
            dve.tensor_scalar(xn[:, b, :], x_res[:, b, :], n.mv[:, b, 0:1], n.rs[:, b:b + 1],
                              ALU.subtract, ALU.mult).then_inc(n.xn_ready, 1)
        dve.wait_ge(ld_c, 48)
        dve.tensor_copy(pick[:, :], pick_raw[:, :]).then_inc(const_ready, 1)
        dve.wait_ge(act_router, 1)
        dve.tensor_copy(ident_b[:, :], ident[:, :]).then_inc(const_ready, 1)
        dve.tensor_tensor(router[1][:, :, 0:NEXP], router_raw[:, :, :], router[0][:, :, 0:NEXP].bitcast(F32),
                          ALU.subtract).then_inc(dve_router, 1)

        def low_gu(p, parity, k):
            dve.wait_ge(act_gu, KT * p + k + 1)
            dve.tensor_tensor(wgu[1][:, parity, k, :], raw_gu[parity][:, k, :], wgu[0][:, parity, k, :].bitcast(F32),
                              ALU.subtract).then_inc(dve_gu, 1)

        def low_d(p, parity, k):
            dve.wait_ge(act_d, 2 * p + k + 1)
            dve.tensor_tensor(wd[1][:, parity, k, :], raw_d[:, parity, k, :], wd[0][:, parity, k, :].bitcast(F32),
                              ALU.subtract).then_inc(dve_d, 1)

        for b in range(NB):
            dve.wait_ge(n.high_ready, b + 1)
            cols = slice(b * P, (b + 1) * P)
            dve.tensor_tensor(act_l[:, :, cols], heads(norm_banks[b % 4][:, :]),
                              act_h[:, :, cols].bitcast(F32), ALU.subtract).then_inc(n.low_ready, 1)

        for pair in range(2):
            for k in range(KT):
                low_gu(pair, pair, k)

        def spread(c):
            return c.unsqueeze(2).broadcast_to([P, NB, NEXP])

        count = [0]

        def done(instruction):
            instruction.then_inc(route, 1)
            count[0] += 1

        top, total, inverse, v1, key1, v2, key2, both = (col[:, i, :] for i in range(8))
        ordered = order[:, :].unsqueeze(1).broadcast_to([P, NB, NEXP])
        dve.wait_ge(pe_logit, 1)
        for half in range(2):
            dve.tensor_copy(logit_row[:, half * HALF:(half + 1) * HALF], ps_u[half][0:NEXP, :]).then_inc(dve_logit, 1)
        dve.wait_ge(pe_logit_turned, 1)
        done(dve.tensor_copy(logit[:, :, :], ps_c[:, 0:NB * NEXP].rearrange("p (b e) -> p b e", b=NB)))
        dve.wait_ge(route, 1)
        done(dve.tensor_reduce(top, logit[:, :, :], AX_X, ALU.max))
        dve.wait_ge(route, 2)
        done(dve.tensor_tensor(rest[:, :, :], logit[:, :, :], spread(top), ALU.subtract))
        dve.wait_ge(act_route, 1)
        done(dve.tensor_reduce(total, prob[:, :, :], AX_X, ALU.add))
        dve.wait_ge(route, 4)
        done(dve.reciprocal(inverse, total))
        dve.wait_ge(route, 5)
        done(dve.tensor_tensor(prob[:, :, :], prob[:, :, :], spread(inverse), ALU.mult))
        left_over = prob
        for best, key, one in ((v1, key1, first_hit), (v2, key2, second_hit)):
            dve.wait_ge(route, count[0])
            done(dve.tensor_reduce(best, left_over[:, :, :], AX_X, ALU.max))
            dve.wait_ge(route, count[0])
            done(dve.tensor_tensor(hit[:, :, :], left_over[:, :, :], spread(best), ALU.is_equal))
            dve.wait_ge(route, count[0])
            done(dve.tensor_tensor(hit[:, :, :], hit[:, :, :], ordered, ALU.mult))
            dve.wait_ge(route, count[0])
            done(dve.tensor_reduce(key, hit[:, :, :], AX_X, ALU.max))
            dve.wait_ge(route, count[0])
            done(dve.tensor_tensor(one[:, :, :], hit[:, :, :], spread(key), ALU.is_equal))
            if best is v1:
                dve.wait_ge(route, count[0])
                done(dve.scalar_tensor_tensor(out=rest[:, :, :], in0=one[:, :, :], scalar=-2.0, in1=prob[:, :, :],
                                              op0=ALU.mult, op1=ALU.add))
                left_over = rest
        dve.wait_ge(route, count[0])
        done(dve.tensor_tensor(weigh[:, :, :], first_hit[:, :, :], second_hit[:, :, :], ALU.add))
        done(dve.tensor_tensor(both, v1, v2, ALU.add))
        dve.wait_ge(route, count[0])
        done(dve.tensor_tensor(weigh[:, :, :], weigh[:, :, :], prob[:, :, :], ALU.mult))
        done(dve.reciprocal(both, both))
        dve.wait_ge(route, count[0])
        dve.wait_ge(zero_ready, 4)
        done(dve.tensor_tensor(comb[:, :, 0:NEXP], weigh[:, :, :], spread(both), ALU.mult))
        for i in range(3):
            piece = pieces[:, :, i * NH:i * NH + NCOMB]
            dve.wait_ge(route, count[0])
            done(dve.tensor_copy(piece, comb[:, :, :]))
            if i < 2:
                dve.wait_ge(route, count[0])
                done(dve.tensor_tensor(comb[:, :, :], comb[:, :, :], piece, ALU.subtract))
        assert count[0] == ROUTE_STEPS
        dve.wait_ge(pe_comb, 1)
        for half in range(2):
            dve.tensor_copy(comb3[:, half * HALF:(half + 1) * HALF], ps_o[half][0:3 * NH, :]).then_inc(comb_ready, 1)

        def body(p, parity, first, last):
            for j in range(STEPS):
                s = STEPS * p + j
                tile = silu[:, j % 2, :]
                dve.wait_ge(act_silu, s + 1)
                dve.wait_ge(pe_c, s + 1)
                dve.tensor_tensor(tile, tile, ps_c[:, :], ALU.mult).then_inc(dve_weighed, 1)
                dve.wait_ge(dve_weighed, s + 1)
                dve.wait_ge(pe_u, s + 1)
                if not at_start(p, j, 2):
                    dve.wait_ge(pool_zl, s - 1)
                dve.tensor_tensor(z[:, j % 2, :], tile, ps_u[j % 2][:, :], ALU.mult).then_inc(dve_z, 1)
                if not (first or last):
                    low_gu(p + 1, 1 - parity, j)
                if not first:
                    accumulate(p - 1, 2 * j)
                    accumulate(p - 1, 2 * j + 1)
                if j < 2:
                    low_d(p, parity, j)

        def accumulate(p, b):
            m = NB * p + b
            dve.wait_ge(pe_o, m + 1)
            if not (isinstance(p, int) and m == 0):
                dve.wait_ge(dve_acc, m)
            dve.tensor_tensor(x_res[:, b, :], x_res[:, b, :], ps_o[b % 2][:, :], ALU.add).then_inc(dve_acc, 1)

        loops(dve, body)
        for b in range(NB):
            accumulate(PAIRS - 1, b)

    @block.tensor
    def _(pe):
        norm_tensor_turn(pe, n, xn, ident, norm_banks)
        pe.wait_ge(dve_router, 1)
        pe.wait_ge(zero_ready, 4)
        for half in range(2):
            pe.wait_ge(n.low_ready, (half + 1) * BPH)
            pe.wait_ge(n.high_ready, (half + 1) * BPH)
            toks = slice(half * HALF, (half + 1) * HALF)
            for k in range(KT):
                mm = product3(pe, ps_u[half][:, :], (router[0][:, k, :], router[1][:, k, :]),
                              (act_h[:, k, toks], act_l[:, k, toks]), k == 0, k == KT - 1)
        mm.then_inc(pe_logit, 1)

        def turn_logits():
            pe.wait_ge(dve_logit, 2)
            for b in range(NB):
                mm = pe.transpose(ps_c[:, b * NEXP:(b + 1) * NEXP], logit_row[:, b * P:(b + 1) * P],
                                  ident[0:NEXP, 0:NEXP])
            mm.then_inc(pe_logit_turned, 1)

        def gate_up(p, parity, j, which):
            s = STEPS * p + j
            bank, used, made = ((ps_g, act_silu, pe_g), (ps_u, dve_z, pe_u))[which]
            if j == 0 and which == 0:
                pe.wait_ge(dve_gu, KT * p + KT)
            if not at_start(p, j, 2):
                pe.wait_ge(used, s - 1)
            toks = slice((j % 2) * HALF, (j % 2 + 1) * HALF)
            cols = slice((2 * (j // 2) + which) * P, (2 * (j // 2) + which + 1) * P)
            for k in range(KT):
                mm = product3(pe, bank[j % 2][:, :], (wgu[0][:, parity, k, cols], wgu[1][:, parity, k, cols]),
                              (act_h[:, k, toks], act_l[:, k, toks]), k == 0, k == KT - 1)
            mm.then_inc(made, 1)

        def combine(p, j):
            s = STEPS * p + j
            if not at_start(p, j):
                pe.wait_ge(dve_weighed, s)
            pe.matmul(ps_c[:, :], pick[:, bass.ds(2 * p + j // 2, 1)].broadcast_to([3 * NH, P]),
                      comb3[:, (j % 2) * HALF:(j % 2 + 1) * HALF], start=True, stop=True).then_inc(pe_c, 1)

        def down(p, parity, b):
            m = NB * p + b
            if b == 0:
                pe.wait_ge(dve_d, 2 * p + 2)
                pe.wait_ge(pool_zl, STEPS * p + STEPS)
            if not (isinstance(p, int) and m < 2):
                pe.wait_ge(dve_acc, m - 1)
            toks = slice(b * P, (b + 1) * P)
            for e in range(2):
                mm = product3(pe, ps_o[b % 2][:, :], (zt[0][:, parity, e, toks], zt[1][:, parity, e, toks]),
                              (wd[0][:, parity, e, :], wd[1][:, parity, e, :]), e == 0, e == 1)
            mm.then_inc(pe_o, 1)

        def body(p, parity, first, last):
            for j in range(STEPS):
                if first and j == 0:
                    gate_up(p, parity, 0, 0)
                    turn_logits()
                    gate_up(p, parity, 0, 1)
                    gate_up(p, parity, 1, 0)
                    gate_up(p, parity, 1, 1)
                    turn_weights()
                if first and j == 1:
                    gate_up(p, parity, 2, 0)
                if not first or j > 2:
                    gate_up(p, parity, j, 0)
                if not first or j > 1:
                    gate_up(p, parity, j, 1)
                combine(p, j)
                if not first:
                    down(p - 1, 1 - parity, 2 * j)
                    down(p - 1, 1 - parity, 2 * j + 1)

        def turn_weights():
            pe.wait_ge(route, ROUTE_STEPS)
            pe.wait_ge(const_ready, 2)
            for b in range(NB):
                mm = pe.matmul(ps_o[b // BPH][0:3 * NH, (b % BPH) * P:(b % BPH + 1) * P], pieces[:, b, :],
                               ident_b[:, :], start=True, stop=True)
            mm.then_inc(pe_comb, 1)
            pe.wait_ge(comb_ready, 2)

        loops(pe, body)
        for b in range(NB):
            down(PAIRS - 1, 1, b)


def decoder_layer(nc, x, context, mask, out, const, w):
    with ExitStack() as ctx:
        x_res = ctx.enter_context(nc.sbuf_tensor("x_res", [P, NB, HID], F32))
        act_h = ctx.enter_context(nc.sbuf_tensor("act_high", [P, KT, NB * P], F32R))
        act_l = ctx.enter_context(nc.sbuf_tensor("act_low", [P, KT, NB * P], F32R))
        ident = ctx.enter_context(nc.sbuf_tensor("ident", [P, P], F32))
        norms = [Norm(lambda name, shape, dt: ctx.enter_context(nc.sbuf_tensor(name, shape, dt)),
                      lambda name: ctx.enter_context(nc.semaphore(name)), tag) for tag in ("self", "ln", "ffn")]
        raw_a = ctx.enter_context(nc.sbuf_tensor("raw_a", [P, KT, (HPG + 1) * P], F32))
        raw_b = ctx.enter_context(nc.sbuf_tensor("raw_b", [P, KT, HALF], F32))
        ld_ctx0, ld_wk, *ld_gu = (ctx.enter_context(nc.semaphore(name)) for name in ("ld_ctx0", "ld_wk", "ld_gu0", "ld_gu1"))
        with ExitStack() as phase:
            self_attention(nc, phase, x_res, act_h, act_l, ident, norms[0:2], raw_a, raw_b, ld_ctx0, ld_wk,
                           const, w, x, context)
        with ExitStack() as phase:
            cross_attention(nc, phase, x_res, act_h, act_l, ident, norms[1:3], raw_a, raw_b,
                            ld_ctx0, ld_wk, ld_gu, const, w, context, mask)
        with ExitStack() as phase:
            experts(nc, phase, x_res, act_h, act_l, ident, norms[2], (raw_a[:, :, 0:HALF], raw_b), ld_gu,
                    const, w, out)


def _lay_out(inputs):
    import numpy as np

    a = {k: np.asarray(v) for k, v in inputs.items()}

    def by_rows(w, groups):
        return w.reshape(groups, -1, KT, P).transpose(0, 3, 2, 1)

    def by_cols(w):
        return w.reshape(HID, NG, HPG, P).transpose(1, 3, 2, 0)

    w = {
        "Wqk": np.concatenate([by_rows(a["L0_attn_Wk"], NG), by_rows(a["L0_attn_Wq"], NG)], axis=3),
        "Wv": by_rows(a["L0_attn_Wv"], 2),
        "Wg": by_rows(a["L0_attn_Wg"], NG),
        "Wo": by_cols(a["L0_attn_Wo"]),
        "Win": by_rows(a["L0_attn_Win"], 1)[0],
        "gnorm": a["L0_attn_gnorm_w"].reshape(P, 1),
        "dt_bias": a["L0_attn_dt_bias"].reshape(NH, 1),
        "A_log": a["L0_attn_A_log_bias"].reshape(NH, 1),
    }
    for m in "qkv":
        w[f"X{m}"] = by_rows(a[f"L0_xattn_w_{m}"], NG)
    w["Xo"] = by_cols(a["L0_xattn_w_out"])
    w["ln_w"] = a["L0_xattn_ln_weight"].reshape(KT, P).T
    w["pos"] = a["L0_xattn_position_bias"].reshape(NG, HPG, P, P).transpose(0, 2, 1, 3)
    gate_up = a["L0_ffn_w_gate_up"].reshape(NEXP, 2, P, HID)
    shared = a["L0_ffn_shared_w_gate_up"].reshape(2, HPG, P, HID).transpose(1, 0, 2, 3)
    w["gu"] = by_rows(np.concatenate([gate_up, shared]), NCOMB // 2)
    down = a["L0_ffn_w_down"].transpose(0, 2, 1)
    shared = a["L0_ffn_shared_w_down"].T.reshape(HPG, P, HID)
    w["down"] = np.concatenate([down, shared]).reshape(NCOMB // 2, 2, P, HID).transpose(0, 2, 1, 3)
    w["router"] = by_rows(a["L0_ffn_gate_w"], 1)[0]
    a["context"] = by_rows(a["ctx_4096"], 2)
    a["mask"] = np.ascontiguousarray(a["mask_BxSxS2_bk0"].transpose(1, 0, 2)).view(np.int32)
    freq = np.float32(1.0) / np.float32(10000.0) ** (np.arange(0, P, 2, dtype=np.float32) / np.float32(P))
    angle = (np.arange(P, dtype=np.float32)[:, None] * freq).T
    key, query = np.arange(P)[:, None], np.arange(P)[None, :]
    const = {
        "ident": np.eye(P, dtype=np.float32),
        "cos": np.concatenate([np.cos(angle), np.cos(angle)]),
        "sin": np.concatenate([-np.sin(angle), np.sin(angle)]),
        "causal": np.tile(np.where(query >= key, 0.0, NEG).astype(np.float32), (1, HPG)),
        "order": np.tile(np.arange(NEXP, 0, -1, dtype=np.float32), (P, 1)),
        "pick": np.tile(np.eye(NH, dtype=np.float32), (3, 1)),
    }
    return a, w, const


def kernel(**inputs):
    import numpy as _np
    import concourse.bacc as _bacc
    from concourse import mybir as _mybir
    from concourse.bass_utils import run_bass_kernel_spmd as _run

    a, w, const = _lay_out(inputs)
    nc = _bacc.Bacc("TRN2", target_bir_lowering=False, num_devices=1)
    arrays = {}

    def dram(name, array):
        arrays[name] = _np.ascontiguousarray(array)
        return nc.dram_tensor(name, arrays[name].shape, _mybir.dt.from_np(arrays[name].dtype), kind="ExternalInput").ap()

    x = dram("in_x", a["x"])
    context, mask = dram("in_context", a["context"]), dram("in_mask", a["mask"])
    w = {k: dram(f"in_{k}", v) for k, v in w.items()}
    const = {k: dram(f"const_{k}", v) for k, v in const.items()}
    out = nc.dram_tensor("out_0", a["x"].shape, _mybir.dt.float32, kind="ExternalOutput").ap()
    decoder_layer(nc, x, context, mask, out, const, w)
    r = _run(nc, [arrays], core_ids=[0])
    return r.results[0]["out_0"]
```
